# Optimizing a Trainium2 kernel written in Bass

```python
import numpy as np
import jax
import jax.numpy as jnp

def _softmax(x, axis=-1):
    return jax.nn.softmax(x, axis=axis)
def _gelu(x):
    return jax.nn.gelu(x, approximate=True)
def _silu(x):
    return jax.nn.silu(x)
def _sigmoid(x):
    return jax.nn.sigmoid(x)
def _layernorm(x, axis=-1, eps=1e-5):
    m = jnp.mean(x, axis=axis, keepdims=True)
    v = jnp.var(x, axis=axis, keepdims=True)
    return (x - m) / jnp.sqrt(v + eps)
def _scatter_add(tgt, idx, src, axis=0):
    return tgt.at[idx].add(src)
def _segment_sum(src, seg, n):
    return jax.ops.segment_sum(src, seg, n)

kernel_name = 'mk_adj_resnorm_d2_adj_128_4d596f'

def setup_inputs(seed: int = 0):
    np.random.seed(seed)
    _w = jnp.asarray
    def _rec_inputs():
        import jax
        import jax.numpy as jnp
        _gk = jax.random.key(seed)
        x = -0.0002928 + 1 * jax.random.normal(jax.random.fold_in(_gk, 1), (32, 512, 128), jnp.float32)
        _a = jax.random.bernoulli(jax.random.fold_in(_gk, 2), 0.0625, (32, 512, 512))
        _a = jnp.logical_or(_a, jnp.eye(512, dtype=bool))
        _af = _a.astype(jnp.float32)
        _af = _af * jax.random.uniform(jax.random.fold_in(_gk, 3), (32, 512, 512), jnp.float32, 0.05, 1)
        adj = _af
        return x, adj
    x, adj = _rec_inputs()
    def _L0_gnn_setup():
        import jax, jax.numpy as jnp
        import numpy as np
        key = jax.random.key(seed)
        k1, k2, k3 = jax.random.split(key, 3)
        B, N, Din, Dout = (8, 4096, 128, 128)
        x = jax.random.normal(k1, (B, N, Din), dtype=jnp.float32)
        adj = jax.random.uniform(k2, (B, N, N), dtype=jnp.float32)
        limit = float(np.sqrt(6.0 / (Din + Dout)))
        weight = jax.random.uniform(k3, (Din, Dout), dtype=jnp.float32, minval=-limit, maxval=limit)
        bias = jnp.zeros((Dout,), dtype=jnp.float32)
        return {'x': x, 'adj': adj, 'weight': weight, 'bias': bias}
    _L0_gnn_all = _L0_gnn_setup()
    _L0_gnn_in = {k: v for k, v in _L0_gnn_all.items() if k in ('weight', 'bias', )}
    del _L0_gnn_all

    def _L1_gnn_setup():
        import jax, jax.numpy as jnp
        import numpy as np
        LN_EPS = 1e-05

        def _layernorm(x, gamma, beta):
            mu = jnp.mean(x, axis=-1, keepdims=True)
            var = jnp.mean(jnp.square(x - mu), axis=-1, keepdims=True)
            return (x - mu) * jax.lax.rsqrt(var + LN_EPS) * gamma + beta
        key = jax.random.key(seed)
        ks = jax.random.split(key, 10)
        B, N, D, O = (2, 512, 128, 128)
        node_features = jax.random.normal(ks[0], (B, N, D), dtype=jnp.float32)
        adjacency = jax.random.uniform(ks[1], (B, N, N), dtype=jnp.float32)
        s1 = 1.0 / np.sqrt(2 * D)
        s2 = 1.0 / np.sqrt(D + O)
        W1 = jax.random.uniform(ks[2], (2 * D, O), jnp.float32, -s1, s1)
        b1 = jax.random.uniform(ks[3], (O,), jnp.float32, -s1, s1)
        g1 = jnp.ones((O,), jnp.float32)
        be1 = jnp.zeros((O,), jnp.float32)
        W2 = jax.random.uniform(ks[4], (D + O, O), jnp.float32, -s2, s2)
        b2 = jax.random.uniform(ks[5], (O,), jnp.float32, -s2, s2)
        g2 = jnp.ones((O,), jnp.float32)
        be2 = jnp.zeros((O,), jnp.float32)
        return {'node_features': node_features, 'adjacency': adjacency, 'W1': W1, 'b1': b1, 'g1': g1, 'be1': be1, 'W2': W2, 'b2': b2, 'g2': g2, 'be2': be2}
    _L1_gnn_all = _L1_gnn_setup()
    _L1_gnn_in = {k: v for k, v in _L1_gnn_all.items() if k in ('W1', 'b1', 'g1', 'be1', 'W2', 'b2', 'g2', 'be2', )}
    del _L1_gnn_all

    return {
        "x": x,
        "adj": adj,
        "L0_gnn_weight": _L0_gnn_in["weight"],
        "L0_gnn_bias": _L0_gnn_in["bias"],
        "L1_gnn_W1": _L1_gnn_in["W1"],
        "L1_gnn_b1": _L1_gnn_in["b1"],
        "L1_gnn_g1": _L1_gnn_in["g1"],
        "L1_gnn_be1": _L1_gnn_in["be1"],
        "L1_gnn_W2": _L1_gnn_in["W2"],
        "L1_gnn_b2": _L1_gnn_in["b2"],
        "L1_gnn_g2": _L1_gnn_in["g2"],
        "L1_gnn_be2": _L1_gnn_in["be2"],
    }

def reference(x, adj, L0_gnn_weight, L0_gnn_bias, L1_gnn_W1, L1_gnn_b1, L1_gnn_g1, L1_gnn_be1, L1_gnn_W2, L1_gnn_b2, L1_gnn_g2, L1_gnn_be2):
    import jax
    import jax.numpy as jnp
    def _L0_gnn_ref(x, adj, weight, bias):
        import jax, jax.numpy as jnp
        import numpy as np
        B, N, _ = x.shape
        adj = adj + jnp.eye(N, dtype=adj.dtype)[None]
        degree = adj.sum(axis=2)
        d_inv_sqrt = degree ** (-0.5)
        d_inv_sqrt = jnp.where(jnp.isinf(d_inv_sqrt), 0.0, d_inv_sqrt)
        adj_norm = d_inv_sqrt[:, :, None] * adj * d_inv_sqrt[:, None, :]
        support = jnp.einsum('bnd,de->bne', x, weight)
        out = jnp.einsum('bnm,bme->bne', adj_norm, support) + bias
        return out

    def _L1_gnn_ref(node_features, adjacency, W1, b1, g1, be1, W2, b2, g2, be2):
        import jax, jax.numpy as jnp
        import numpy as np
        LN_EPS = 1e-05

        def _layernorm(x, gamma, beta):
            mu = jnp.mean(x, axis=-1, keepdims=True)
            var = jnp.mean(jnp.square(x - mu), axis=-1, keepdims=True)
            return (x - mu) * jax.lax.rsqrt(var + LN_EPS) * gamma + beta
        B, N, D = node_features.shape
        m_j = jnp.einsum('bnd,do->bno', node_features, W1[:D])
        m_i = jnp.einsum('bnd,do->bno', node_features, W1[D:])
        pre = m_j[:, None, :, :] + m_i[:, :, None, :] + b1
        msg = jax.nn.gelu(_layernorm(pre, g1, be1), approximate=False)
        agg = jnp.einsum('bijo,bij->bio', msg, adjacency)
        upd_in = jnp.concatenate([node_features, agg], axis=-1)
        updated = _layernorm(upd_in @ W2 + b2, g2, be2)
        return updated

    x = _layernorm(x + _L0_gnn_ref(x, adj, L0_gnn_weight, L0_gnn_bias), axis=-1)
    x = _layernorm(x + _L1_gnn_ref(x, adj, L1_gnn_W1, L1_gnn_b1, L1_gnn_g1, L1_gnn_be1, L1_gnn_W2, L1_gnn_b2, L1_gnn_g2, L1_gnn_be2), axis=-1)
    return x


_drawn_inputs = setup_inputs


def setup_inputs(seed=0):
    import zlib

    import numpy as np

    out = dict(_drawn_inputs(seed))
    spreads = {'L0_gnn_bias': (0.0, 0.1),
     'L1_gnn_g1': (1.0, 0.2),
     'L1_gnn_be1': (0.0, 0.1),
     'L1_gnn_g2': (1.0, 0.2),
     'L1_gnn_be2': (0.0, 0.1)}
    factors = {'L1_gnn_b2': 6.485}
    for name, (base, spread) in spreads.items():
        noise = np.random.default_rng([zlib.crc32(name.encode()), seed]).standard_normal(out[name].shape)
        drawn = base * np.exp(spread * noise) if base else spread * noise
        out[name] = jnp.asarray(drawn.astype(out[name].dtype))
    for name, factor in factors.items():
        out[name] = (out[name] * factor).astype(out[name].dtype)
    return out
```

```python
from contextlib import ExitStack

import numpy as np
import concourse.bass as bass
from concourse import mybir

FP32 = mybir.dt.float32
BF16 = mybir.dt.bfloat16
U32 = mybir.dt.uint32
I32 = mybir.dt.int32
ALU = mybir.AluOpType
ACT = mybir.ActivationFunctionType
AX = mybir.AxisListType

B, N, D = 32, 512, 128
P = 128
TB = N // P
TILES = B * TB
SLOTS = 8
PRIMARY = 7
ALWAYS = 4
XR = 4
EPS = 1e-5
RSQRT_OPS = 12
MAGIC = float(0x5F3759DF)


def adj_resnorm_kernel(nc, x, adj, w0, b0, w1, b1, g1, be1, w2, b2, g2, be2, out):
    x_rows = x.rearrange("b (t p) d -> b p t d", p=P)
    adj_rows = adj.rearrange("b (t p) m -> b p t m", p=P)
    adj_tiles = adj.rearrange("b n m -> (b n) m")
    out_rows = out.rearrange("b n d -> (b n) d")
    row = lambda v: v.rearrange("(a n) -> a n", a=1)

    ctx = ExitStack()
    with ctx:
        def sb(name, shape, dt=FP32):
            return ctx.enter_context(nc.sbuf_tensor(name, shape, dt))

        def sem(name):
            return ctx.enter_context(nc.semaphore(name))

        msg_j = nc.dram_tensor("msg_j", [B * N, D], FP32).ap()
        own = nc.dram_tensor("own", [B * N, 3 * D], FP32).ap()

        ident = sb("ident", [P, P])
        w0_sb = sb("w0_sb", [P, D])
        w1_sb = sb("w1_sb", [P, 2, D])
        w2_sb = sb("w2_sb", [P, 2, D])
        vecs = sb("vecs", [P, 7, D])
        b0_all, b1_all, g1_all, be1_all, b2_all, g2_all, be2_all = (vecs[:, k, :] for k in range(7))
        mean1 = sb("mean1", [P, 3])
        parts = sb("parts", [P, 3, 2 * D], BF16)
        rest = sb("rest", [P, 2 * D])
        split = sb("split", [3, 2 * D], BF16)
        be1_split = sb("be1_split", [3, 4, D], BF16)
        ones3 = sb("ones3", [3, P], BF16)
        base = sb("base", [P, TILES])

        adj_g = sb("adj_g", [P, 2, TB, N])
        x_g = sb("x_g", [P, 2, TB, D])
        xb_g = sb("xb_g", [P, TB, D])
        xT = sb("xT", [P, N])
        deg = sb("deg", [P, TB])
        dis = sb("dis", [P, TB])
        nonzero = sb("nonzero", [P, TB])
        sup = sb("sup", [P, TB, D])
        adjT = sb("adjT", [P, TB, N])
        stats_g = sb("stats_g", [P, TB, 6])
        mv_g = sb("mv_g", [P, TB, 2])
        own_g = sb("own_g", [P, 2, TB, 3 * D])
        h_g = sb("h_g", [P, TB, D])
        pre_g = sb("pre_g", [P, TB, D])
        mj_g = sb("mj_g", [P, 2, TB, D])
        junk_a = sb("junk_a", [P, TB, N], BF16)
        junk_v = sb("junk_v", [P, 2, TB, N], BF16)
        counts = sb("counts", [P, 2, TILES])
        most = sb("most", [P, 4])
        chunk_row = sb("chunk_row", [1, 4, TILES])
        chunk_int = sb("chunk_int", [1, 4, TILES], I32)
        POS, OVER_POS, OVER_NEG, OVER = range(4)

        rs_v = sb("rs_v", [P, SLOTS])
        rs_i = sb("rs_i", [P, SLOTS], U32)
        rs_u = sb("rs_u", [P, SLOTS])

        adj_t = sb("adj_t", [P, 2, N])
        key = sb("key", [P, 2, N])
        own_t = sb("own_t", [P, 2, 3 * D])
        weight = sb("weight", [P, 2, PRIMARY * SLOTS])
        found = sb("found", [P, 2, PRIMARY * SLOTS], U32)
        index = sb("index", [P, 2, PRIMARY * SLOTS], U32)
        gathered = sb("gathered", [P, 2, PRIMARY * SLOTS, D])
        pre = sb("pre", [P, XR, SLOTS, D])
        squares = sb("squares", [P, 2, SLOTS, D])
        ssq = sb("ssq", [P, 2, SLOTS])
        rstd = sb("rstd", [P, 2, SLOTS])
        msg = sb("msg", [P, 2, SLOTS, D])
        agg_sb = sb("agg_sb", [P, 4, D])
        aggT_sb = sb("aggT_sb", [P, P])
        upd = sb("upd", [P, D])
        res = sb("res", [P, D])
        stats = sb("stats", [P, 6])
        mv = sb("mv", [P, 2])
        rs_t = sb("rs_t", [P, 1])
        out_sb = sb("out_sb", [P, 2, D])

        o_weight = sb("o_weight", [P, SLOTS])
        o_found = sb("o_found", [P, SLOTS], U32)
        o_index = sb("o_index", [P, SLOTS], U32)
        o_gathered = sb("o_gathered", [P, SLOTS, D])

        bank = [ctx.enter_context(nc.psum_tensor(f"bank{k}", [P, 512], FP32)) for k in range(4)]
        zbank = [ctx.enter_context(nc.psum_tensor(f"zbank{k}", [P, 2, 512], FP32)) for k in range(2)]

        s_const = sem("s_const")
        s_carrier = {e.engine: sem(f"s_carrier{k}") for k, e in enumerate((nc.sync, nc.gpsimd, nc.vector))}
        s_ident = sem("s_ident")
        s_iota = sem("s_iota")
        s_seq = sem("s_seq")
        s_setup = sem("s_setup")
        g_load = [sem(f"g_load{q}") for q in range(2)]
        g_xb = sem("g_xb")
        g_xT = sem("g_xT")
        g_xTc = sem("g_xTc")
        g_deg = sem("g_deg")
        g_count = sem("g_count")
        g_dis = sem("g_dis")
        g_sup = sem("g_sup")
        g_supc = sem("g_supc")
        g_adjT = sem("g_adjT")
        g_adjTa = sem("g_adjTa")
        g_adjTv = sem("g_adjTv")
        g_prod = sem("g_prod")
        g_pre = sem("g_pre")
        g_h = sem("g_h")
        g_hb = sem("g_hb")
        g_hT = sem("g_hT")
        g_hTc = sem("g_hTc")
        g_m = sem("g_m")
        g_mj = sem("g_mj")
        g_mi = sem("g_mi")
        g_rs = sem("g_rs")
        g_seq = sem("g_seq")
        g_store = [sem(f"g_store{q}") for q in range(2)]
        c_rows = sem("c_rows")
        c_most = sem("c_most")
        c_ready = sem("c_ready")

        t_adj = [sem(f"t_adj{q}") for q in range(2)]
        t_own = [sem(f"t_own{q}") for q in range(2)]
        t_key = sem("t_key")
        t_max = sem("t_max")
        t_idx = sem("t_idx")
        t_find = sem("t_find")
        t_zap = sem("t_zap")
        t_gather = [sem(f"t_gather{c}") for c in range(PRIMARY)]
        t_pre = sem("t_pre")
        t_ssq = sem("t_ssq")
        t_rs = sem("t_rs")
        t_scaled = sem("t_scaled")
        t_z = sem("t_z")
        t_msg = sem("t_msg")
        t_wmsg = sem("t_wmsg")
        t_agg = sem("t_agg")
        t_over = sem("t_over")
        t_overpe = sem("t_overpe")
        e_agg = sem("e_agg")
        e_aggT = sem("e_aggT")
        e_aggTc = sem("e_aggTc")
        e_upd = sem("e_upd")
        e_seq = sem("e_seq")
        e_bn = sem("e_bn")
        e_out = sem("e_out")
        e_store = [sem(f"e_store{q}") for q in range(2)]
        o_key = sem("o_key")
        o_seq = sem("o_seq")
        o_idx = sem("o_idx")
        o_dma = sem("o_dma")
        o_gather = sem("o_gather")
        o_pre = sem("o_pre")
        o_ssq = sem("o_ssq")
        o_scaled = sem("o_scaled")
        o_z = sem("o_z")
        o_msg = sem("o_msg")
        o_wmsg = sem("o_wmsg")
        o_agg = sem("o_agg")

        block = ctx.enter_context(nc.Block())

        N_CONST = 3 + 7
        over_slots = PRIMARY * SLOTS

        def wait_alone(eng, sem, value):
            eng.wait_ge(sem, value)
            eng.sem_inc(s_carrier[eng.engine], 1)

        def before(c, ring):
            return (c - ring, 0) if c >= ring else (max(k for k in range(PRIMARY) if k % ring == c % ring), 1)

        def tile_loop(eng, body, ahead=0):
            body(0, 0, True, False)
            body(1, 1, False, False)
            with eng.Fori(1, TILES // 2 - 1) as pair:
                t = eng.snap(pair * 2)
                body(t, 0, False, False)
                body(t + 1, 1, False, False)
            body(TILES - 2, 0, False, False)
            body(TILES - 1, 1, False, True)

        def uses(t, q):
            return (t - q) // 2 if isinstance(t, int) else (t - q) >> 1

        @block.sync
        def _(sp):
            sp.dma_start(w0_sb[:, :], w0).then_inc(s_const, 16)
            sp.dma_start(w1_sb[:, :, :], w1.rearrange("(k p) o -> p k o", p=P)).then_inc(s_const, 16)
            sp.dma_start(w2_sb[:, :, :], w2.rearrange("(k p) o -> p k o", p=P)).then_inc(s_const, 16)
            for k, v in enumerate((b0, b1, g1, be1, b2, g2, be2)):
                sp.dma_start(vecs[:, k, :], row(v).partition_broadcast(P)).then_inc(s_const, 16)

            def load_graph(b, q, fresh):
                if not fresh:
                    wait_alone(sp, g_pre, b - 1)
                    wait_alone(sp, g_adjT, 4 * (b - 1))
                    wait_alone(sp, g_deg, b - 1)
                    wait_alone(sp, g_count, b - 1)
                sp.dma_start(x_g[:, q, :, :], x_rows[b]).then_inc(g_load[q], 16)
                sp.dma_start(adj_g[:, q, :, :], adj_rows[b]).then_inc(g_load[q], 16)

            def store_graph(b, q):
                wait_alone(sp, g_mj, b + 1)
                wait_alone(sp, g_mi, b + 1)
                wait_alone(sp, g_hb, b + 1)
                rows = bass.ds(b * N, N)
                sp.dma_start(msg_j[rows, :].rearrange("(t p) d -> p t d", p=P), mj_g[:, q, :, :]).then_inc(g_store[q], 16)
                sp.dma_start(own[rows, :].rearrange("(t p) d -> p t d", p=P), own_g[:, q, :, :]).then_inc(g_store[q], 16)

            load_graph(0, 0, True)
            load_graph(1, 1, True)
            with sp.Fori(0, B // 2 - 1) as pair:
                b = sp.snap(pair * 2)
                store_graph(b, 0)
                load_graph(b + 2, 0, False)
                store_graph(b + 1, 1)
                load_graph(b + 3, 1, False)
            store_graph(B - 2, 0)
            store_graph(B - 1, 1)
            for q in range(2):
                sp.wait_ge(g_store[q], 32 * (B // 2))

            def load_adj(t, q):
                sp.dma_start(adj_t[:, q, :], adj_tiles[bass.ds(t * P, P), :]).then_inc(t_adj[q], 16)

            def load_own(t, q):
                sp.dma_start(own_t[:, q, :], own[bass.ds(t * P, P), :]).then_inc(t_own[q], 16)

            for q in range(2):
                load_adj(q, q)
                load_own(q, q)

            def tile(t, q, first, last):
                if not last and not (isinstance(t, int) and t == TILES - 2):
                    wait_alone(sp, t_over, t + 1)
                    load_adj(t + 2, q)
                if not first:
                    finish(t - 1, 1 - q, last)

            def finish(t, q, last):
                wait_alone(sp, e_out, t + 1)
                sp.dma_start(out_rows[bass.ds(t * P, P), :], out_sb[:, q, :]).then_inc(e_store[q], 16)
                if not last:
                    load_own(t + 2, q)

            tile_loop(sp, tile)
            finish(TILES - 1, 1, True)
            for q in range(2):
                sp.wait_ge(e_store[q], 16 * (TILES // 2))

        @block.gpsimd
        def _(pool):
            pool.memset(ident[:, :], 0.0).then_inc(s_ident, 1)
            pool.wait_ge(s_ident, 1)
            pool.affine_select(out=ident[:, :], in_=ident[:, :], compare_op=ALU.not_equal, fill=1.0,
                               base=0, pattern=[[-1, P]], channel_multiplier=1).then_inc(s_ident, 1)
            pool.iota(base[:, :], [[N, B], [0, TB]], base=0, channel_multiplier=0,
                      allow_small_or_imprecise_dtypes=True).then_inc(s_iota, 1)
            pool.memset(gathered[:, :, :, :], 0.0).then_inc(s_iota, 1)
            pool.wait_ge(s_const, 16 * N_CONST)
            pool.wait_ge(s_setup, 1)

            def graph(b, q):
                wait_alone(pool, g_load[q], 32 * (uses(b, q) + 1))
                if not (isinstance(b, int) and b == 0):
                    wait_alone(pool, g_pre, b)
                pool.tensor_tensor(xb_g[:, :, :], x_g[:, q, :, :],
                                   b0_all.unsqueeze(1).to_broadcast([P, TB, D]), ALU.add).then_inc(g_xb, 1)
                wait_alone(pool, g_h, b + 1)
                pool.tensor_tensor(own_g[:, q, :, 0:D], h_g[:, :, :],
                                   be2_all.unsqueeze(1).to_broadcast([P, TB, D]), ALU.add).then_inc(g_hb, 1)

            graph(0, 0)
            graph(1, 1)
            with pool.Fori(1, B // 2) as pair:
                b = pool.snap(pair * 2)
                graph(b, 0)
                graph(b + 1, 1)
            for q in range(2):
                pool.wait_ge(g_store[q], 32 * (B // 2))
            pool.wait_ge(c_ready, 1)

            seen = pool.alloc_register("pool_overflow_seen")
            pool.reg_mov(seen, 0)

            def gather(chunk, into, idx, done):
                for j in range(SLOTS):
                    pool.indirect_dma_start(into[:, chunk * SLOTS + j, :], None, msg_j,
                                            bass.IndirectOffsetOnAxis(ap=idx[:, chunk * SLOTS + j:chunk * SLOTS + j + 1], axis=0)
                                            ).then_inc(done, 16)

            def tile(t, q, first, last):
                longest = pool.value_load(chunk_int[0:1, POS, bass.ds(t, 1)], min_val=0, max_val=N)
                for c in range(PRIMARY):
                    wait_alone(pool, t_idx, t * PRIMARY + c + 1)
                    if not (isinstance(t, int) and t < 2):
                        wait_alone(pool, t_pre, (t - 2) * PRIMARY + c + 1)
                    if c < ALWAYS:
                        gather(c, gathered[:, q, :, :], index[:, q, :], t_gather[c])
                    else:
                        with pool.If(longest > c * SLOTS):
                            gather(c, gathered[:, q, :, :], index[:, q, :], t_gather[c])
                over = pool.value_load(chunk_int[0:1, OVER, bass.ds(t, 1)], min_val=0, max_val=2 * N // SLOTS)
                with pool.If(over > 0):
                    with pool.Fori(0, over):
                        k = pool.snap(seen)
                        wait_alone(pool, o_idx, k + 1)
                        gather(0, o_gathered[:, :, :], o_index[:, :], o_dma)
                        wait_alone(pool, o_dma, (k + 1) * (16 * SLOTS))
                        pool.sem_inc(o_gather, 1)
                        pool.reg_add(seen, seen, 1)

            tile_loop(pool, tile)

        @block.scalar
        def _(act):
            act.wait_ge(s_ident, 2)

            def graph(b, q):
                act.wait_ge(g_load[q], 32 * (uses(b, q) + 1))
                if not (isinstance(b, int) and b == 0):
                    act.wait_ge(g_dis, b)
                for it in range(TB):
                    done = act.activation(junk_a[:, it, :], adj_g[:, q, it, :], ACT.Identity,
                                          accum_out=deg[:, it:it + 1])
                done.then_inc(g_deg, 1)
                act.wait_ge(g_xT, b + 1)
                if not (isinstance(b, int) and b == 0):
                    act.wait_ge(g_sup, b)
                act.copy(xT[:, :], bank[0][:, :]).then_inc(g_xTc, 1)
                for mt in range(2):
                    act.wait_ge(g_adjT, 4 * b + mt + 1)
                    if not (isinstance(b, int) and b == 0):
                        act.wait_ge(g_prod, b)
                    act.copy(adjT[:, mt, :], zbank[0][:, mt, :]).then_inc(g_adjTa, 1)
                act.wait_ge(g_hT, b + 1)
                if not (isinstance(b, int) and b < 2):
                    act.wait_ge(g_store[q], 32 * uses(b, q))
                act.copy(own_g[:, q, :, 2 * D:3 * D], bank[0][:, :].rearrange("p (t n) -> p t n", t=TB)).then_inc(g_hTc, 1)
                act.wait_ge(g_m, b + 1)
                act.copy(mj_g[:, q, :, :], zbank[0][:, 0, :].rearrange("p (t o) -> p t o", t=TB)).then_inc(g_mj, 1)

            graph(0, 0)
            graph(1, 1)
            with act.Fori(1, B // 2) as pair:
                b = act.snap(pair * 2)
                graph(b, 0)
                graph(b + 1, 1)
            act.wait_ge(c_ready, 1)

            seen = act.alloc_register("act_overflow_seen")
            act.reg_mov(seen, 0)

            def positive(t, q):
                act.wait_ge(t_adj[q], 16 * (uses(t, q) + 1))
                act.activation(key[:, q, :], adj_t[:, q, :], ACT.Relu).then_inc(t_key, 1)

            positive(0, 0)

            def sums_of_squares(src, c, done):
                for j in range(SLOTS):
                    last = act.activation(squares[:, c % 2, j, :], src[:, j, :], ACT.Square,
                                          accum_out=ssq[:, c % 2, j:j + 1])
                last.then_inc(done, 1)

            def epilogue_sum(t, q):
                act.wait_ge(t_overpe, t + 1)
                if not (isinstance(t, int) and t == 0):
                    act.wait_ge(e_aggT, t)
                act.copy(agg_sb[:, :, :], bank[q][:, :].rearrange("p (k o) -> p k o", k=4)).then_inc(e_agg, 1)

            def epilogue_transposed(t, q):
                act.wait_ge(e_aggT, t + 1)
                act.copy(aggT_sb[:, :], bank[2][:, 0:P]).then_inc(e_aggTc, 1)

            def tile(t, q, first, last):
                n = t * PRIMARY
                for s in range(PRIMARY + 2):
                    if s < PRIMARY:
                        c = s
                        act.wait_ge(t_pre, n + c + 1)
                        prev, back = before(c, 2)
                        if not (first and back):
                            act.wait_ge(t_rs, ((t - back) * PRIMARY + prev + 1) * RSQRT_OPS)
                            act.wait_ge(t_ssq, (t - back) * PRIMARY + prev + 1)
                        sums_of_squares(pre[:, c % XR, :, :], c, t_ssq)
                    if 0 <= s - 2:
                        c = s - 2
                        act.wait_ge(t_z, n + c + 1)
                        prev, back = before(c, 2)
                        if not (first and back):
                            act.wait_ge(t_agg, (t - back) * PRIMARY + prev + 1)
                        act.activation(msg[:, c % 2, :, :], zbank[c % 2][:, :, :].rearrange("p h (s o) -> p (h s) o", s=4),
                                       ACT.Gelu).then_inc(t_msg, 1)
                    if s == 0 and not first:
                        epilogue_sum(t - 1, 1 - q)
                    if s == 1 and not first:
                        epilogue_transposed(t - 1, 1 - q)
                    if s == 0 and not last:
                        if not first:
                            act.wait_ge(t_over, t)
                        positive(t + 1, 1 - q)
                over = act.value_load(chunk_int[0:1, OVER, bass.ds(t, 1)], min_val=0, max_val=2 * N // SLOTS)
                with act.If(over > 0):
                    act.wait_ge(t_agg, n + PRIMARY)
                    with act.Fori(0, over):
                        k = act.snap(seen)
                        act.wait_ge(o_pre, k + 1)
                        sums_of_squares(pre[:, 0, :, :], 0, o_ssq)
                        act.wait_ge(o_z, k + 1)
                        act.activation(msg[:, 0, :, :], zbank[0][:, :, :].rearrange("p h (s o) -> p (h s) o", s=4),
                                       ACT.Gelu).then_inc(o_msg, 1)
                        act.reg_add(seen, seen, 1)

            tile_loop(act, tile)
            epilogue_sum(TILES - 1, 1)
            epilogue_transposed(TILES - 1, 1)

        @block.vector
        def _(dve):
            steps = [0]

            def step(ins):
                steps[0] += 1
                ins.then_inc(s_seq, 1)
                dve.wait_ge(s_seq, steps[0])

            def rsqrt_op(j, v, y, n, eps, done):
                vv, ii, uu = rs_v[:, 0:n], rs_i[:, 0:n], rs_u[:, 0:n]
                if j == 0:
                    ins = dve.tensor_scalar(vv, v, eps, None, ALU.add)
                elif j == 1:
                    ins = dve.tensor_scalar(ii, vv.bitcast(U32), 1, None, ALU.logical_shift_right)
                elif j == 2:
                    ins = dve.tensor_scalar(y.bitcast(U32), ii, -1.0, MAGIC, ALU.mult, ALU.add)
                elif j % 3 == 0:
                    ins = dve.scalar_tensor_tensor(uu, y, -0.5, y, ALU.mult, ALU.mult)
                elif j % 3 == 1:
                    ins = dve.tensor_tensor(uu, uu, vv, ALU.mult)
                else:
                    ins = dve.scalar_tensor_tensor(y, uu, 1.5, y, ALU.add, ALU.mult)
                ins.then_inc(done, 1)

            dve.wait_ge(s_const, 16 * N_CONST)
            dve.wait_ge(s_ident, 2)
            for k in range(2):
                step(dve.reduce_sum(mean1[:, k:k + 1], w1_sb[:, k, :], AX.X))
            step(dve.reduce_sum(mean1[:, 2:3], b1_all, AX.X))
            step(dve.tensor_scalar(mean1[:, :], mean1[:, :], -1.0 / D, None, ALU.mult))
            for k in range(2):
                step(dve.tensor_scalar(w1_sb[:, k, :], w1_sb[:, k, :], mean1[:, k:k + 1], None, ALU.add))
            step(dve.tensor_scalar(b1_all, b1_all, mean1[:, 2:3], None, ALU.add))
            step(dve.tensor_scalar(g1_all, g1_all, float(np.float32(np.sqrt(D))), None, ALU.mult))
            step(dve.tensor_copy(rest[:, :], vecs[:, 3:5, :].rearrange("p k d -> p (k d)")))
            for k in range(3):
                step(dve.tensor_copy(parts[:, k, :], rest[:, :]))
                step(dve.tensor_tensor(rest[:, :], rest[:, :], parts[:, k, :], ALU.subtract))
            step(dve.tensor_scalar(split[:, :], parts[0:3, 0, :], ident[0:3, 0:1], None, ALU.mult))
            for k in (1, 2):
                step(dve.scalar_tensor_tensor(split[:, :], parts[0:3, k, :], ident[0:3, k:k + 1], split[:, :], ALU.mult, ALU.add))
            step(dve.tensor_copy(be1_split[:, :, :], split[:, 0:D].unsqueeze(1).to_broadcast([3, 4, D])))
            step(dve.memset(ones3[:, :], 1.0))
            dve.sem_inc(s_setup, 1)

            GSEQ = 3
            def graph(b, q):
                dve.wait_ge(g_load[q], 32 * (uses(b, q) + 1))
                if not (isinstance(b, int) and b == 0):
                    dve.wait_ge(g_count, b)
                for it in range(TB):
                    for sign, op in enumerate((ALU.is_gt, ALU.is_lt)):
                        last = dve.tensor_scalar(junk_v[:, sign, it, :], adj_g[:, q, it, :], 0.0, 0.0, op, ALU.add,
                                                 accum_out=counts[:, sign, bass.ds(b * TB + it, 1)])
                last.then_inc(g_count, 1)
                dve.wait_ge(g_deg, b + 1)
                for j in range(RSQRT_OPS):
                    if j:
                        dve.wait_ge(g_rs, 2 * RSQRT_OPS * b + j)
                    rsqrt_op(j, deg[:, :], dis[:, :], TB, 1.0, g_rs)
                dve.wait_ge(g_rs, 2 * RSQRT_OPS * b + RSQRT_OPS)
                dve.tensor_scalar(nonzero[:, :], rs_v[:, 0:TB], 0.0, None, ALU.not_equal).then_inc(g_seq, 1)
                dve.wait_ge(g_seq, GSEQ * b + 1)
                dve.tensor_tensor(dis[:, :], dis[:, :], nonzero[:, :], ALU.mult).then_inc(g_dis, 1)
                dve.wait_ge(g_dis, b + 1)
                dve.wait_ge(g_sup, b + 1)
                dve.tensor_tensor(sup[:, :, :], bank[1][:, :].rearrange("p (t d) -> p t d", t=TB),
                                  dis[:, :].unsqueeze(2).to_broadcast([P, TB, D]), ALU.mult).then_inc(g_supc, 1)
                for mt in range(2):
                    dve.wait_ge(g_adjT, 4 * b + mt + 3)
                    dve.tensor_copy(adjT[:, mt + 2, :], zbank[1][:, mt, :]).then_inc(g_adjTv, 1)
                dve.wait_ge(g_prod, b + 1)
                dve.wait_ge(g_xb, b + 1)
                for it in range(TB):
                    last = dve.scalar_tensor_tensor(pre_g[:, it, :], bank[2][:, it * D:(it + 1) * D], dis[:, it:it + 1],
                                                    xb_g[:, it, :], ALU.mult, ALU.add)
                last.then_inc(g_pre, 1)
                dve.wait_ge(g_pre, b + 1)
                for it in range(TB):
                    last = dve.bn_stats(stats_g[:, it, :], pre_g[:, it, :])
                last.then_inc(g_seq, 1)
                wait_alone(dve, g_seq, GSEQ * b + 2)
                for it in range(TB):
                    last = dve.bn_aggr(mv_g[:, it, :], stats_g[:, it, :])
                last.then_inc(g_seq, 1)
                dve.wait_ge(g_seq, GSEQ * b + 3)
                for j in range(RSQRT_OPS):
                    dve.wait_ge(g_rs, 2 * RSQRT_OPS * b + RSQRT_OPS + j)
                    rsqrt_op(j, mv_g[:, :, 1], nonzero[:, :], TB, EPS, g_rs)
                dve.wait_ge(g_rs, 2 * RSQRT_OPS * (b + 1))
                if not (isinstance(b, int) and b == 0):
                    dve.wait_ge(g_hb, b)
                for it in range(TB):
                    last = dve.tensor_scalar(h_g[:, it, :], pre_g[:, it, :], mv_g[:, it, 0:1], nonzero[:, it:it + 1],
                                             ALU.subtract, ALU.mult)
                last.then_inc(g_h, 1)
                dve.wait_ge(g_m, b + 1)
                if not (isinstance(b, int) and b < 2):
                    dve.wait_ge(g_store[q], 32 * uses(b, q))
                dve.tensor_tensor(own_g[:, q, :, D:2 * D], zbank[0][:, 1, :].rearrange("p (t o) -> p t o", t=TB),
                                  b1_all.unsqueeze(1).to_broadcast([P, TB, D]), ALU.add).then_inc(g_mi, 1)

            graph(0, 0)
            graph(1, 1)
            with dve.Fori(1, B // 2) as pair:
                b = dve.snap(pair * 2)
                graph(b, 0)
                graph(b + 1, 1)

            dve.wait_ge(c_rows, 1)
            for sign in range(2):
                step(dve.reduce_max(most[:, sign:sign + 1], bank[0][:, sign * P:(sign + 1) * P], AX.X))
            step(dve.tensor_scalar(most[:, 2:3], most[:, 0:1], float(over_slots), float(SLOTS - 1 - over_slots), ALU.max, ALU.add))
            step(dve.tensor_scalar(most[:, 3:4], most[:, 1:2], float(SLOTS - 1), None, ALU.add))
            dve.sem_inc(c_most, 1)
            dve.wait_ge(c_rows, 2)
            step(dve.tensor_copy(chunk_int[0:1, 0, :], bank[1][0:1, 0:P]))
            for k in (OVER_POS, OVER_NEG):
                step(dve.tensor_copy(chunk_int[0:1, k, :], bank[1][0:1, (k + 1) * P:(k + 2) * P]))
                step(dve.tensor_scalar(chunk_int[0:1, k, :], chunk_int[0:1, k, :], 3, None, ALU.logical_shift_right))
            step(dve.tensor_tensor(chunk_int[0:1, OVER, :], chunk_int[0:1, OVER_POS, :], chunk_int[0:1, OVER_NEG, :], ALU.add))
            dve.sem_inc(c_ready, 1)
            dve.wait_ge(s_iota, 2)

            seen = dve.alloc_register("dve_overflow_seen")
            dve.reg_mov(seen, 0)
            gathers = [dve.alloc_register(f"dve_gathers{c}") for c in range(ALWAYS, PRIMARY)]
            for reg in gathers:
                dve.reg_mov(reg, 0)

            def search_max(t, q, c):
                if c == 0:
                    wait_alone(dve, t_key, t + 1)
                else:
                    wait_alone(dve, t_zap, t * PRIMARY + c)
                dve.max(weight[:, q, c * SLOTS:(c + 1) * SLOTS], key[:, q, :]).then_inc(t_max, 1)

            def search_index(t, q, c):
                at = slice(c * SLOTS, (c + 1) * SLOTS)
                wait_alone(dve, t_max, t * PRIMARY + c + 1)
                dve.max_index(found[:, q, at], weight[:, q, at], key[:, q, :]).then_inc(t_find, 1)
                dve.match_replace(out=key[:, q, :], in_to_replace=weight[:, q, at], in_values=key[:, q, :],
                                  imm_value=0.0).then_inc(t_zap, 1)
                dve.wait_ge(t_find, t * PRIMARY + c + 1)
                dve.tensor_scalar(index[:, q, at], found[:, q, at], base[:, bass.ds(t, 1)], None, ALU.add).then_inc(t_idx, 1)

            for c in range(PRIMARY):
                search_max(0, 0, c)
                search_index(0, 0, c)

            def add_own(dst, src, q, done):
                dve.tensor_tensor(dst, src, own_t[:, q, D:2 * D].unsqueeze(1).to_broadcast([P, SLOTS, D]),
                                  ALU.add).then_inc(done, 1)

            def scale_slot(xs, c, j):
                return dve.scalar_tensor_tensor(pre[:, xs, j, :], pre[:, xs, j, :], rstd[:, c % 2, j:j + 1], g1_all,
                                                ALU.mult, ALU.mult)

            ESEQ = 6 + RSQRT_OPS * 2
            def epilogue(t, q):
                def link(ins):
                    count[0] += 1
                    ins.then_inc(e_seq, 1)
                    wait_alone(dve, e_seq, t * ESEQ + count[0])
                count = [0]
                dve.wait_ge(e_upd, t + 1)
                u = bank[2][:, P:2 * P]
                link(dve.bn_stats(stats[:, :], u))
                link(dve.bn_aggr(mv[:, :], stats[:, :]))
                for j in range(RSQRT_OPS):
                    count[0] += 1
                    rsqrt_op(j, mv[:, 1:2], rs_t[:, :], 1, EPS, e_seq)
                    dve.wait_ge(e_seq, t * ESEQ + count[0])
                link(dve.tensor_scalar(upd[:, :], u, mv[:, 0:1], rs_t[:, :], ALU.subtract, ALU.mult))
                link(dve.tensor_tensor(res[:, :], upd[:, :], g2_all, ALU.mult))
                link(dve.tensor_tensor(res[:, :], res[:, :], own_t[:, q, 0:D], ALU.add))
                link(dve.bn_stats(stats[:, :], res[:, :]))
                dve.bn_aggr(mv[:, :], stats[:, :]).then_inc(e_bn, 1)
                dve.wait_ge(e_bn, t + 1)
                for j in range(RSQRT_OPS):
                    count[0] += 1
                    rsqrt_op(j, mv[:, 1:2], rs_t[:, :], 1, EPS, e_seq)
                    dve.wait_ge(e_seq, t * ESEQ + count[0])
                if not (isinstance(t, int) and t < 2):
                    dve.wait_ge(e_store[q], 16 * uses(t, q))
                dve.tensor_scalar(out_sb[:, q, :], res[:, :], mv[:, 0:1], rs_t[:, :], ALU.subtract, ALU.mult).then_inc(e_out, 1)

            def overflow_chunk(q, sign):
                k = dve.snap(seen)
                def link(ins):
                    count[0] += 1
                    ins.then_inc(o_seq, 1)
                    wait_alone(dve, o_seq, k * OSEQ + count[0])
                count = [0]
                link(dve.max(o_weight[:, :], key[:, q, :]))
                link(dve.max_index(o_found[:, :], o_weight[:, :], key[:, q, :]))
                link(dve.match_replace(out=key[:, q, :], in_to_replace=o_weight[:, :], in_values=key[:, q, :], imm_value=0.0))
                link(dve.tensor_scalar(o_weight[:, :], o_weight[:, :], sign, None, ALU.mult))
                dve.tensor_scalar(o_index[:, :], o_found[:, :], base[:, bass.ds(t_now[0], 1)], None, ALU.add).then_inc(o_idx, 1)
                dve.wait_ge(o_gather, k + 1)
                add_own(pre[:, 0, :, :], o_gathered[:, :, :], q, o_pre)
                dve.wait_ge(o_ssq, k + 1)
                for j in range(RSQRT_OPS):
                    count[0] += 1
                    rsqrt_op(j, ssq[:, 0, :], rstd[:, 0, :], SLOTS, D * EPS, o_seq)
                    dve.wait_ge(o_seq, k * OSEQ + count[0])
                for j in range(SLOTS):
                    last = scale_slot(0, 0, j)
                last.then_inc(o_scaled, 1)
                dve.wait_ge(o_msg, k + 1)
                dve.tensor_tensor(msg[:, 0, :, :], msg[:, 0, :, :], o_weight[:, :].unsqueeze(2).to_broadcast([P, SLOTS, D]),
                                  ALU.mult).then_inc(o_wmsg, 1)
                dve.wait_ge(o_agg, k + 1)
                dve.reg_add(seen, seen, 1)
            OSEQ = 4 + RSQRT_OPS
            t_now = [0]

            def tile(t, q, first, last):
                n = t * PRIMARY
                t_now[0] = t
                longest = dve.value_load(chunk_int[0:1, POS, bass.ds(t, 1)], min_val=0, max_val=N)
                dve.wait_ge(t_own[q], 16 * (uses(t, q) + 1))
                for s in range(PRIMARY + 3):
                    if s < PRIMARY:
                        c = s
                        if c < ALWAYS:
                            dve.wait_ge(t_gather[c], (t + 1) * (16 * SLOTS))
                        else:
                            with dve.If(longest > c * SLOTS):
                                done = dve.snap(gathers[c - ALWAYS])
                                wait_alone(dve, t_gather[c], (done + 1) * (16 * SLOTS))
                                dve.reg_add(gathers[c - ALWAYS], gathers[c - ALWAYS], 1)
                        prev, back = before(c, XR)
                        if not (first and back):
                            dve.wait_ge(t_z, (t - back) * PRIMARY + prev + 1)
                        add_own(pre[:, c % XR, :, :], gathered[:, q, c * SLOTS:(c + 1) * SLOTS, :], q, t_pre)
                    if 0 <= s - 3:
                        c = s - 3
                        dve.wait_ge(t_msg, n + c + 1)
                        dve.tensor_tensor(msg[:, c % 2, :, :], msg[:, c % 2, :, :],
                                          weight[:, q, c * SLOTS:(c + 1) * SLOTS].unsqueeze(2).to_broadcast([P, SLOTS, D]),
                                          ALU.mult).then_inc(t_wmsg, 1)
                    if 1 <= s <= PRIMARY and not last:
                        search_max(t + 1, 1 - q, s - 1)
                    roots, scales = 0 <= s - 1 < PRIMARY, 0 <= s - 2 < PRIMARY
                    if roots:
                        dve.wait_ge(t_ssq, n + s)
                    for j in range(RSQRT_OPS):
                        if scales and j < SLOTS:
                            done = scale_slot((s - 2) % XR, s - 2, j)
                            if j == SLOTS - 1:
                                done.then_inc(t_scaled, 1)
                        if roots:
                            if j:
                                dve.wait_ge(t_rs, (n + s - 1) * RSQRT_OPS + j)
                            rsqrt_op(j, ssq[:, (s - 1) % 2, :], rstd[:, (s - 1) % 2, :], SLOTS, D * EPS, t_rs)
                    if 1 <= s <= PRIMARY and not last:
                        search_index(t + 1, 1 - q, s - 1)
                    if roots:
                        wait_alone(dve, t_rs, (n + s) * RSQRT_OPS)
                    if s == 3 and not first:
                        epilogue(t - 1, 1 - q)
                wait_alone(dve, t_wmsg, n + PRIMARY)
                over = dve.value_load(chunk_int[0:1, OVER_POS, bass.ds(t, 1)], min_val=0, max_val=N // SLOTS)
                with dve.If(over > 0):
                    with dve.Fori(0, over):
                        overflow_chunk(q, 1.0)
                over = dve.value_load(chunk_int[0:1, OVER_NEG, bass.ds(t, 1)], min_val=0, max_val=N // SLOTS)
                with dve.If(over > 0):
                    dve.tensor_scalar(key[:, q, :], adj_t[:, q, :], -1.0, 0.0, ALU.mult, ALU.max).then_inc(o_key, 1)
                    dve.wait_ge(o_key, 1)
                    dve.sem_clear(o_key)
                    with dve.Fori(0, over):
                        overflow_chunk(q, -1.0)
                dve.sem_inc(t_over, 1)

            tile_loop(dve, tile)
            epilogue(TILES - 1, 1)

        @block.tensor
        def _(pe):
            pe.wait_ge(s_ident, 2)
            pe.wait_ge(s_setup, 1)
            mm = nc.tensor.matmul

            def graph(b, q):
                pe.wait_ge(g_load[q], 32 * (uses(b, q) + 1))
                if not (isinstance(b, int) and b == 0):
                    pe.wait_ge(g_hTc, b)
                for it in range(TB):
                    last = nc.tensor.transpose(bank[0][:, it * P:(it + 1) * P], x_g[:, q, it, :], ident[:, :])
                last.then_inc(g_xT, 1)
                if not (isinstance(b, int) and b == 0):
                    pe.wait_ge(g_mj, b)
                    pe.wait_ge(g_mi, b)
                for mt in range(TB):
                    for it in range(TB):
                        last = nc.tensor.transpose(zbank[mt // 2][:, mt % 2, it * P:(it + 1) * P],
                                                   adj_g[:, q, it, mt * P:(mt + 1) * P], ident[:, :])
                    last.then_inc(g_adjT, 1)
                pe.wait_ge(g_xTc, b + 1)
                for it in range(TB):
                    last = mm(bank[1][:, it * D:(it + 1) * D], xT[:, it * P:(it + 1) * P], w0_sb[:, :], start=True, stop=True)
                last.then_inc(g_sup, 1)
                pe.wait_ge(g_supc, b + 1)
                pe.wait_ge(g_adjTa, 2 * b + 2)
                pe.wait_ge(g_adjTv, 2 * b + 2)
                for it in range(TB):
                    dst = bank[2][:, it * D:(it + 1) * D]
                    for mt in range(TB):
                        mm(dst, adjT[:, mt, it * P:(it + 1) * P], sup[:, mt, :], start=(mt == 0), stop=False)
                    last = mm(dst, ident[:, :], sup[:, it, :], start=False, stop=True)
                last.then_inc(g_prod, 1)
                pe.wait_ge(g_h, b + 1)
                for it in range(TB):
                    last = nc.tensor.transpose(bank[0][:, it * P:(it + 1) * P], h_g[:, it, :], ident[:, :])
                last.then_inc(g_hT, 1)
                pe.wait_ge(g_hTc, b + 1)
                for it in range(TB):
                    for k in range(2):
                        last = mm(zbank[0][:, k, it * D:(it + 1) * D], own_g[:, q, it, 2 * D:3 * D], w1_sb[:, k, :],
                                  start=True, stop=True)
                last.then_inc(g_m, 1)

            graph(0, 0)
            graph(1, 1)
            with pe.Fori(1, B // 2) as pair:
                b = pe.snap(pair * 2)
                graph(b, 0)
                graph(b + 1, 1)

            pe.wait_ge(g_count, B)
            pe.wait_ge(g_hTc, B)
            for sign in range(2):
                last = nc.tensor.transpose(bank[0][:, sign * P:(sign + 1) * P], counts[:, sign, :], ident[:, :])
            last.then_inc(c_rows, 1)
            pe.wait_ge(c_most, 1)
            for k in range(4):
                last = mm(bank[1][0:1, k * P:(k + 1) * P], most[:, k:k + 1], ident[:, :], start=True, stop=True)
            last.then_inc(c_rows, 1)
            pe.wait_ge(c_ready, 1)

            seen = pe.alloc_register("pe_overflow_seen")
            pe.reg_mov(seen, 0)

            def normed(xs, z, done):
                for half in range(2):
                    mm(zbank[z][:, half, :], ident[:, :], pre[:, xs, 4 * half:4 * half + 4, :].rearrange("p s o -> p (s o)"),
                       start=True, stop=False)
                    last = mm(zbank[z][:, half, :], ones3[:, :], be1_split[:, :, :].rearrange("p s o -> p (s o)"),
                              start=False, stop=True)
                last.then_inc(done, 1)

            def accumulate(m, q, start, done):
                for half in range(2):
                    last = mm(bank[q][:, :], ident[:, :], msg[:, m, 4 * half:4 * half + 4, :].rearrange("p s o -> p (s o)"),
                              start=(start and half == 0), stop=True, skip_group_check=True)
                last.then_inc(done, 1)

            def epilogue_transposed(t, q):
                pe.wait_ge(e_agg, t + 1)
                if not (isinstance(t, int) and t == 0):
                    pe.wait_ge(e_out, t)
                for k in range(4):
                    last = mm(bank[2][:, 0:P], agg_sb[:, k, :], ident[:, :], start=(k == 0), stop=(k == 3))
                last.then_inc(e_aggT, 1)

            def epilogue_update(t, q):
                pe.wait_ge(e_aggTc, t + 1)
                u = bank[2][:, P:2 * P]
                mm(u, own_t[:, q, 2 * D:3 * D], w2_sb[:, 0, :], start=True, stop=False)
                mm(u, aggT_sb[:, :], w2_sb[:, 1, :], start=False, stop=False)
                mm(u, ones3[:, :], split[:, D:2 * D], start=False, stop=True).then_inc(e_upd, 1)

            def tile(t, q, first, last):
                n = t * PRIMARY
                for s in range(PRIMARY + 1):
                    if s < PRIMARY:
                        c = s
                        pe.wait_ge(t_scaled, n + c + 1)
                        prev, back = before(c, 2)
                        if not (first and back):
                            pe.wait_ge(t_msg, (t - back) * PRIMARY + prev + 1)
                        normed(c % XR, c % 2, t_z)
                    if s == 0 and not first:
                        epilogue_transposed(t - 1, 1 - q)
                    if s == 1 and not first:
                        epilogue_update(t - 1, 1 - q)
                    if s >= 1:
                        c = s - 1
                        pe.wait_ge(t_wmsg, n + c + 1)
                        if c == 0 and not (isinstance(t, int) and t < 2):
                            pe.wait_ge(e_agg, t - 1)
                        accumulate(c % 2, q, c == 0, t_agg)
                over = pe.value_load(chunk_int[0:1, OVER, bass.ds(t, 1)], min_val=0, max_val=2 * N // SLOTS)
                with pe.If(over > 0):
                    with pe.Fori(0, over):
                        k = pe.snap(seen)
                        pe.wait_ge(o_scaled, k + 1)
                        normed(0, 0, o_z)
                        pe.wait_ge(o_wmsg, k + 1)
                        accumulate(0, q, False, o_agg)
                        pe.wait_ge(o_agg, k + 1)
                        pe.reg_add(seen, seen, 1)
                pe.wait_ge(t_agg, n + PRIMARY)
                pe.sem_inc(t_overpe, 1)

            tile_loop(pe, tile)
            epilogue_transposed(TILES - 1, 1)
            epilogue_update(TILES - 1, 1)


INS = ["x", "adj", "L0_gnn_weight", "L0_gnn_bias", "L1_gnn_W1", "L1_gnn_b1", "L1_gnn_g1", "L1_gnn_be1",
       "L1_gnn_W2", "L1_gnn_b2", "L1_gnn_g2", "L1_gnn_be2"]


def kernel(**inputs):
    import concourse.bacc as bacc
    from concourse.bass_utils import run_bass_kernel_spmd

    nc = bacc.Bacc("TRN2", target_bir_lowering=False, num_devices=1)
    arrays = {f"in_{n}": np.ascontiguousarray(inputs[n]) for n in INS}
    args = [nc.dram_tensor(n, a.shape, mybir.dt.from_np(a.dtype), kind="ExternalInput").ap() for n, a in arrays.items()]
    out = nc.dram_tensor("out_0", (B, N, D), FP32, kind="ExternalOutput").ap()
    adj_resnorm_kernel(nc, *args, out)
    r = run_bass_kernel_spmd(nc, [arrays], core_ids=[0])
    return r.results[0]["out_0"]
```

```python
from contextlib import ExitStack

import numpy as np
import concourse.bass as bass
from concourse import mybir

FP32 = mybir.dt.float32
BF16 = mybir.dt.bfloat16
U32 = mybir.dt.uint32
I32 = mybir.dt.int32
ALU = mybir.AluOpType
ACT = mybir.ActivationFunctionType
AX = mybir.AxisListType

B, N, D = 32, 512, 128
P = 128
TB = N // P
TILES = B * TB
SLOTS = 8
CHUNKS = (7, 5, 5, 4)
STARTS = (0, 7, 12, 17)
G = sum(CHUNKS)
MAYBE = ((0, 5), (0, 6), (1, 4), (2, 3), (2, 4), (3, 3))
AHEAD = 6
RING = 7
RG = 3
EPS = 1e-5
MAGIC = float(0x5F3759DF)
STEPS = 11
ROOT_D = float(np.float32(np.sqrt(D)))


def tile_of(i):
    j = i % G
    k = max(k for k in range(TB) if STARTS[k] <= j)
    return k, j - STARTS[k]


def adj_resnorm_kernel(nc, x, adj, w0, b0, w1, b1, g1, be1, w2, b2, g2, be2, out):
    x_rows = x.rearrange("b (t p) d -> b p t d", p=P)
    adj_rows = adj.rearrange("b (t p) m -> b p t m", p=P)
    adj_flat = adj.rearrange("b n m -> (b n) m")
    out_flat = out.rearrange("b n d -> (b n) d")

    ctx = ExitStack()
    with ctx:
        def sb(name, shape, dt=FP32):
            return ctx.enter_context(nc.sbuf_tensor(name, shape, dt))

        def sem(name):
            return ctx.enter_context(nc.semaphore(name))

        msg_j = nc.dram_tensor("msg_j", [B * N, D], FP32).ap()
        own = nc.dram_tensor("own", [B * N, 2 * D], FP32).ap()

        ident = sb("ident", [P, P])
        w0_sb = sb("w0_sb", [P, D])
        w1_sb = sb("w1_sb", [P, 2, D])
        w2_sb = sb("w2_sb", [P, 2, D])
        vecs = sb("vecs", [P, 5, D])
        b0_all, b1_all, b2_all, g2_all, be2_all = (vecs[:, k, :] for k in range(5))
        cols = sb("cols", [P, 2])
        mean1 = sb("mean1", [P, 3])
        parts = sb("parts", [P, 3, D], BF16)
        rest = sb("rest", [P, D])
        b2_split = sb("b2_split", [3, D], BF16)
        ones3 = sb("ones3", [3, P], BF16)
        base = sb("base", [P, TILES])
        number = sb("number", [P, TB])
        backward = sb("backward", [P, TB])
        places = sb("places", [P, N])

        adj_g = sb("adj_g", [P, 2, TB, N])
        x_g = sb("x_g", [P, 2, TB, D])
        xb_g = sb("xb_g", [P, 2, TB, D])
        xT = sb("xT", [P, N])
        deg = sb("deg", [P, TB])
        nv = sb("nv", [P, 2 * TB])
        ny = sb("ny", [P, 2 * TB])
        ni = sb("ni", [P, 2 * TB], U32)
        nu = sb("nu", [P, 2 * TB])
        nonzero = sb("nonzero", [P, TB])
        dis = sb("dis", [P, TB])
        sup = sb("sup", [P, TB, D])
        adjT = sb("adjT", [P, TB, N])
        pre_g = sb("pre_g", [P, TB, D])
        stats_g = sb("stats_g", [P, TB, 6])
        mv_g = sb("mv_g", [P, TB, 2])
        own_g = sb("own_g", [P, 2, TB, 2 * D])
        hT = sb("hT", [P, N])
        mj_g = sb("mj_g", [P, 2, TB, D])
        junk_a = sb("junk_a", [P, TB, N], BF16)
        junk_v = sb("junk_v", [P, 3, TB, N], BF16)
        count_g = sb("count_g", [P, 2, TB])
        sort_key = sb("sort_key", [P, TB])
        rank = sb("rank", [P, TB])
        chosen = sb("chosen", [P, TB, N])
        reach = sb("reach", [P, TB, TB])
        row_id = sb("row_id", [P, TILES], U32)
        counts = sb("counts", [P, 2, TILES])
        most = sb("most", [P, 2])
        longest_f = sb("longest_f", [1, 2, B, TB])
        sized = sb("sized", [1, B])
        summed = sb("summed", [1, B])
        zeros = sb("zeros", [1, B])
        longest_i = sb("longest_i", [1, 4, B, TB], I32)
        LONGEST, OVER_POS, OVER_NEG, OVER = range(4)
        arrivals = sb("arrivals", [1, len(MAYBE), B], I32)

        adj_t = sb("adj_t", [P, TB, N])
        key = sb("key", [P, TB, N])
        ids_adj = sb("ids_adj", [P, TB], U32)
        ids_row = sb("ids_row", [P, TB], U32)
        own_t = sb("own_t", [P, TB, 2 * D])
        weight = sb("weight", [P, G, SLOTS])
        found = sb("found", [P, G, SLOTS], U32)
        index = sb("index", [P, G, SLOTS], U32)
        gathered = sb("gathered", [P, RING * SLOTS, D])
        pre = sb("pre", [P, RG, SLOTS, D])
        squares = sb("squares", [P, RG, SLOTS, D], BF16)
        ssq = sb("ssq", [P, RG, SLOTS + 1])
        rstd = sb("rstd", [P, RG, SLOTS + 1])
        rs_v = sb("rs_v", [P, SLOTS + 1])
        rs_i = sb("rs_i", [P, SLOTS + 1], U32)
        rs_u = sb("rs_u", [P, SLOTS + 1])
        msgT = sb("msgT", [P, RG, SLOTS, P])
        msg = sb("msg", [P, RG, SLOTS, D])
        agg_sb = sb("agg_sb", [P, 4, D])
        endT = sb("endT", [P, 2, P])
        upd = sb("upd", [P, D])
        res = sb("res", [P, D])
        stats = sb("stats", [P, 6])
        mv = sb("mv", [P, 2])
        r_end = sb("r_end", [P, 1])
        out_sb = sb("out_sb", [P, 2, D])
        o_weight = sb("o_weight", [P, SLOTS])
        o_found = sb("o_found", [P, SLOTS], U32)
        o_index = sb("o_index", [P, SLOTS], U32)
        o_pre = sb("o_pre", [P, SLOTS, D])
        o_squares = sb("o_squares", [P, SLOTS, D], BF16)
        o_ssq = sb("o_ssq", [P, SLOTS])
        o_rstd = sb("o_rstd", [P, SLOTS])
        o_msgT = sb("o_msgT", [P, SLOTS, P])
        o_msg = sb("o_msg", [P, SLOTS, D])

        def pb(name, banks):
            return ctx.enter_context(nc.psum_tensor(name, [P, banks, 512], FP32))
        xT_ps = pb("xT_ps", 1)
        sup_ps = pb("sup_ps", 1)
        prod_ps = pb("prod_ps", 1)
        hT_ps = pb("hT_ps", 1)
        adjT_ps = pb("adjT_ps", 2)
        adjT2_ps = pb("adjT2_ps", 2)
        agg_ps = (xT_ps, sup_ps)
        end_ps, o_ps, zt_ps, zb_ps = prod_ps, hT_ps, adjT_ps, adjT2_ps

        s_const, s_ident, s_iota, s_zero, s_seq, s_setup, s_rows, s_most, s_ready = (
            sem(f"s_{n}") for n in ("const", "ident", "iota", "zero", "seq", "setup", "rows", "most", "ready"))
        g_load = [sem(f"g_load{q}") for q in range(2)]
        g_store = [sem(f"g_store{q}") for q in range(2)]
        (g_xb, g_xT, g_xTc, g_deg, g_count, g_key, g_keys, g_nv, g_dis, g_sup, g_supc, g_adjT, g_adjTa, g_adjTv,
         g_prod, g_pre, g_stats, g_rs, g_mask, g_h, g_hT, g_hTc, g_m, g_mj, g_mi, g_rank, g_reach, g_chosen, g_order,
         g_ids) = (
            sem(f"g_{n}") for n in ("xb", "xT", "xTc", "deg", "count", "key", "keys", "nv", "dis", "sup", "supc", "adjT",
                                    "adjTa", "adjTv", "prod", "pre", "stats", "rs", "mask", "h", "hT", "hTc", "m", "mj",
                                    "mi", "rank", "reach", "chosen", "order", "ids"))
        t_adj = [sem(f"t_adj{k}") for k in range(TB)]
        t_own = [sem(f"t_own{k}") for k in range(TB)]
        t_rows = [sem(f"t_rows{r}") for r in range(RING)]
        t_maybe = [sem(f"t_maybe{m}") for m in range(len(MAYBE))]
        t_ids_adj, t_ids_row = sem("t_ids_adj"), sem("t_ids_row")
        (t_key, t_max, t_find, t_zap, t_idx, t_pre, t_ssq, t_rs, t_scaled, t_zt, t_gelu, t_zb, t_wmsg, t_agg, t_over,
         t_sum) = (sem(f"t_{n}") for n in ("key", "max", "find", "zap", "idx", "pre", "ssq", "rs", "scaled", "zt", "gelu",
                                           "zb", "wmsg", "agg", "over", "sum"))
        e_agg, e_T, e_Tc, e_upd, e_seq, e_var, e_root, e_out = (
            sem(f"e_{n}") for n in ("agg", "T", "Tc", "upd", "seq", "var", "root", "out"))
        e_store = [sem(f"e_store{q}") for q in range(2)]
        o_key, o_seq, o_idx, o_dma, o_rows, o_prep, o_sums, o_root, o_scaled, o_zt, o_gelu, o_zb, o_wmsg, o_agg = (
            sem(f"o_{n}") for n in ("key", "seq", "idx", "dma", "rows", "prep", "sums", "root", "scaled", "zt", "gelu",
                                    "zb", "wmsg", "agg"))
        s_carrier = {e.engine: sem(f"s_carrier{k}") for k, e in enumerate((nc.sync, nc.gpsimd, nc.vector))}

        block = ctx.enter_context(nc.Block())
        N_CONST = 3 + 5 + 2
        E_STEPS = 9

        def wait_alone(eng, sem, value):
            eng.wait_ge(sem, value)
            eng.sem_inc(s_carrier[eng.engine], 1)

        def graph_loop(eng, body):
            body(0, 0, True, False)
            with eng.Fori(0, (B - 2) // 2) as pair:
                b = eng.snap(pair * 2)
                body(b + 1, 1, True, True)
                body(b + 2, 0, True, True)
            body(B - 1, 1, True, True)
            body(B, 0, False, True)

        def chunk_loop(eng, steps, until, lead=0):
            def graph(b, first, last):
                def known(i, off=0):
                    return not (first and i - off < 0) and not (last and i - off >= G)
                bG = b * G if isinstance(b, int) else eng.snap(b * G)
                for i in range(-lead if first else 0, until if last else G):
                    steps(b, bG, i, known)
            graph(0, True, False)
            with eng.Fori(1, B - 1) as b:
                graph(b, False, False)
            graph(B - 1, False, True)

        def ends(i, off):
            k, c = tile_of(i - off)
            return k if c == CHUNKS[k] - 1 else None

        def begins(i, off):
            k, c = tile_of(i - off)
            return k if c == 0 else None

        def stored(b, q):
            return 16 * (b - q)

        def graph_of(b, i, off):
            return b + (i - off) // G

        def tiles_before(b, i, off):
            return b * TB + (i - off) // G * TB + tile_of(i - off)[0]

        @block.sync
        def _(sp):
            sp.dma_start(w0_sb[:, :], w0).then_inc(s_const, 16)
            sp.dma_start(w1_sb[:, :, :], w1.rearrange("(k p) o -> p k o", p=P)).then_inc(s_const, 16)
            sp.dma_start(w2_sb[:, :, :], w2.rearrange("(k p) o -> p k o", p=P)).then_inc(s_const, 16)
            for k, v in enumerate((b0, b1, b2, g2, be2)):
                sp.dma_start(vecs[:, k, :], v.rearrange("(a n) -> a n", a=1).partition_broadcast(P)).then_inc(s_const, 16)
            for k, v in enumerate((g1, be1)):
                sp.dma_start(cols[:, k:k + 1], v.rearrange("(n a) -> n a", a=1)).then_inc(s_const, 16)

            def graph(b, q, front, back):
                if front:
                    if not (isinstance(b, int) and b < 2):
                        wait_alone(sp, g_xb, b - 1)
                        wait_alone(sp, g_xT, b - 1)
                        wait_alone(sp, g_adjT, 4 * (b - 1))
                        wait_alone(sp, g_deg, b - 1)
                        wait_alone(sp, g_count, b - 1)
                    sp.dma_start(x_g[:, q, :, :], x_rows[b]).then_inc(g_load[q], 16)
                    sp.dma_start(adj_g[:, q, :, :], adj_rows[b]).then_inc(g_load[q], 16)
                if back:
                    wait_alone(sp, g_mj, b)
                    wait_alone(sp, g_mi, b)
                    rows = bass.ds((b - 1) * N, N)
                    sp.dma_start(msg_j[rows, :].rearrange("(t p) d -> p t d", p=P), mj_g[:, 1 - q, :, :]).then_inc(g_store[1 - q], 16)
                    sp.dma_start(own[rows, :].rearrange("(t p) d -> p t d", p=P), own_g[:, 1 - q, :, :]).then_inc(g_store[1 - q], 16)

            graph_loop(sp, graph)

        @block.gpsimd
        def _(pool):
            pool.memset(ident[:, :], 0.0).then_inc(s_ident, 1)
            pool.wait_ge(s_ident, 1)
            pool.affine_select(out=ident[:, :], in_=ident[:, :], compare_op=ALU.not_equal, fill=1.0,
                               base=0, pattern=[[-1, P]], channel_multiplier=1).then_inc(s_ident, 1)
            for tensor, pattern, start, step in ((base, [[N, B], [0, TB]], 0, 0), (number, [[P, TB]], 0, 1),
                                                 (backward, [[-P, TB]], N - 1, -1), (places, [[1, N]], 0, 0)):
                pool.iota(tensor[:, :], pattern, base=start, channel_multiplier=step,
                          allow_small_or_imprecise_dtypes=True).then_inc(s_iota, 1)
            pool.memset(gathered[:, :, :], 0.0).then_inc(s_zero, 1)
            pool.memset(ssq[:, :, :], 1.0).then_inc(s_zero, 1)
            pool.wait_ge(s_const, 16 * N_CONST)

            def graph(b, q, front, back):
                if front:
                    wait_alone(pool, g_load[q], 16 * b + (32 if q == 0 else 16))
                    if not (isinstance(b, int) and b < 2):
                        wait_alone(pool, g_pre, b - 1)
                    pool.tensor_tensor(xb_g[:, q, :, :], x_g[:, q, :, :],
                                       b0_all.unsqueeze(1).to_broadcast([P, TB, D]), ALU.add).then_inc(g_xb, 1)

            graph_loop(pool, graph)
            for q in range(2):
                pool.wait_ge(g_store[q], 32 * (B // 2))
            pool.wait_ge(s_ready, 1)

            seen = pool.alloc_register("pool_overflow_seen")
            pool.reg_mov(seen, 0)

            def rows_of(source, into, idx, done):
                pool.indirect_dma_start(into, None, source, bass.IndirectOffsetOnAxis(ap=idx, axis=0)).then_inc(done, 16)

            def copy_ids(into, t, k, copied):
                pool.tensor_copy(into[:, k:k + 1], row_id[:, bass.ds(t, 1)]).then_inc(copied, 1)
                wait_alone(pool, copied, t + 1)
                return into[:, k:k + 1]

            def adj_of(b, i, off):
                t, k = tiles_before(b, i, off), tile_of(i - off)[0]
                if not (isinstance(t, int) and t < TB):
                    wait_alone(pool, t_adj[k], 16 * graph_of(b, i, off))
                    wait_alone(pool, t_over, t - TB + 1)
                rows_of(adj_flat, adj_t[:, k, :], copy_ids(ids_adj, t, k, t_ids_adj), t_adj[k])

            def own_of(b, i, off):
                t, k = tiles_before(b, i, off), tile_of(i - off)[0]
                if not (isinstance(t, int) and t < TB):
                    wait_alone(pool, e_out, t - TB + 1)
                    wait_alone(pool, e_store[k % 2], 8 * (t - k % 2) - 16)
                rows_of(own, own_t[:, k, :], copy_ids(ids_row, t, k, t_ids_row), t_own[k])

            for i in range(-8, 0):
                if begins(i, -8) is not None:
                    adj_of(0, i, -8)
                if begins(i, -2) is not None and i + 2 >= 0:
                    own_of(0, i, -2)

            def steps(b, bG, i, known):
                if begins(i, -8) is not None and known(i, -8):
                    adj_of(b, i, -8)
                if begins(i, -2) is not None and known(i, -2):
                    own_of(b, i, -2)
                if known(i):
                    k, c = tile_of(i)
                    wait_alone(pool, t_idx, bG + i + 1)
                    if known(i, RING):
                        wait_alone(pool, t_pre, bG + i - RING + 1)
                    at = i % RING * SLOTS
                    def slot(j, done):
                        rows_of(msg_j, gathered[:, at + j, :], index[:, i, j:j + 1], done)
                    if (k, c) not in MAYBE:
                        for j in range(SLOTS):
                            slot(j, t_rows[i % RING])
                    else:
                        m = MAYBE.index((k, c))
                        longest = pool.value_load(longest_i[0:1, LONGEST, bass.ds(b, 1), k], min_val=0, max_val=N)
                        with pool.If(longest > c * SLOTS):
                            slot(0, t_maybe[m])
                            for j in range(1, SLOTS):
                                with pool.If(longest > c * SLOTS + j):
                                    slot(j, t_maybe[m])
                k = ends(i, 3)
                if k is not None and known(i, 3):
                    d = (i - 3) // G
                    over = pool.value_load(longest_i[0:1, OVER, bass.ds(b + d, 1), k], min_val=0, max_val=2 * N // SLOTS)
                    with pool.If(over > 0):
                        with pool.Fori(0, over):
                            n = pool.snap(seen)
                            wait_alone(pool, o_idx, n + 1)
                            for j in range(SLOTS):
                                rows_of(msg_j, o_pre[:, j, :], o_index[:, j:j + 1], o_dma)
                            wait_alone(pool, o_dma, (n + 1) * (16 * SLOTS))
                            pool.sem_inc(o_rows, 1)
                            pool.reg_add(seen, seen, 1)
                k = ends(i, 12)
                if k is not None and known(i, 12):
                    t = tiles_before(b, i, 12)
                    wait_alone(pool, e_out, t + 1)
                    pool.indirect_dma_start(out_flat, bass.IndirectOffsetOnAxis(ap=ids_row[:, k:k + 1], axis=0), out_sb[:, k % 2, :],
                                            None).then_inc(e_store[k % 2], 16)

            chunk_loop(pool, steps, G + 12)
            for q in range(2):
                pool.wait_ge(e_store[q], 16 * (TILES // 2))

        @block.scalar
        def _(act):
            def graph(b, q, front, back):
                if front:
                    act.wait_ge(g_load[q], 16 * b + (32 if q == 0 else 16))
                    if not (isinstance(b, int) and b == 0):
                        act.wait_ge(g_nv, b)
                    for it in range(TB):
                        last = act.activation(junk_a[:, it, :], adj_g[:, q, it, :], ACT.Identity, accum_out=deg[:, it:it + 1])
                    last.then_inc(g_deg, 1)
                    act.wait_ge(g_xT, b + 1)
                    if not (isinstance(b, int) and b == 0):
                        act.wait_ge(g_sup, b)
                    act.copy(xT[:, :], xT_ps[:, 0, :]).then_inc(g_xTc, 1)
                    for mt in range(2):
                        act.wait_ge(g_adjT, 4 * b + mt + 1)
                        if not (isinstance(b, int) and b == 0):
                            act.wait_ge(g_prod, b)
                        act.copy(adjT[:, mt, :], adjT_ps[:, mt, :]).then_inc(g_adjTa, 1)
                if back:
                    act.wait_ge(g_hT, b)
                    if not (isinstance(b, int) and b < 2):
                        act.wait_ge(g_m, b - 1)
                    act.copy(hT[:, :], hT_ps[:, 0, :]).then_inc(g_hTc, 1)
                    act.wait_ge(g_m, b)
                    if not (isinstance(b, int) and b < 3):
                        act.wait_ge(g_store[1 - q], stored(b - 1, 1 - q))
                    act.copy(mj_g[:, 1 - q, :, :], adjT_ps[:, 0, :].rearrange("p (t o) -> p t o", t=TB)).then_inc(g_mj, 1)

            graph_loop(act, graph)
            act.wait_ge(s_ready, 1)
            act.wait_ge(s_zero, 2)

            seen = act.alloc_register("act_overflow_seen")
            act.reg_mov(seen, 0)

            def steps(b, bG, i, known):
                if known(i):
                    act.wait_ge(t_pre, bG + i + 1)
                    if known(i, RG):
                        act.wait_ge(t_rs, (bG + i - RG + 1) * (STEPS + 1))
                        act.wait_ge(t_ssq, bG + i - RG + 1)
                    for j in range(SLOTS):
                        last = act.activation(squares[:, i % RG, j, :], pre[:, i % RG, j, :], ACT.Square,
                                              accum_out=ssq[:, i % RG, j:j + 1])
                    last.then_inc(t_ssq, 1)
                k = ends(i, 4)
                if k is not None and known(i, 4):
                    t = tiles_before(b, i, 4)
                    act.wait_ge(t_sum, t + 1)
                    if not (isinstance(t, int) and t == 0):
                        act.wait_ge(e_T, t)
                    act.copy(agg_sb[:, :, :], agg_ps[k % 2][:, 0, :].rearrange("p (k o) -> p k o", k=4)).then_inc(e_agg, 1)
                k = begins(i, -7)
                if k is not None and known(i, -7):
                    d = (i + 7) // G
                    t = tiles_before(b, i, -7)
                    act.wait_ge(t_adj[k], (b + d + 1) * 16)
                    if not (isinstance(t, int) and t < TB):
                        act.wait_ge(t_over, t - TB + 1)
                    act.activation(key[:, k, :], adj_t[:, k, :], ACT.Relu).then_inc(t_key, 1)
                if known(i, 2):
                    act.wait_ge(t_zt, bG + i - 1)
                    if known(i, 2 + RG):
                        act.wait_ge(t_zb, bG + i - 1 - RG)
                    act.activation(msgT[:, (i - 2) % RG, :, :], zt_ps[:, :, :].rearrange("p h (s n) -> p (h s) n", s=4),
                                   ACT.Gelu, bias=cols[:, 1:2], scale=cols[:, 0:1]).then_inc(t_gelu, 1)
                if known(i, 1):
                    act.wait_ge(t_rs, (bG + i) * (STEPS + 1))
                    for j in range(SLOTS):
                        r = (i - 1) % RG
                        last = act.activation(pre[:, r, j, :], pre[:, r, j, :], ACT.Identity, scale=rstd[:, r, j:j + 1])
                    last.then_inc(t_scaled, 1)
                k = ends(i, 5)
                if k is not None and known(i, 5):
                    act.wait_ge(e_T, tiles_before(b, i, 5) + 1)
                    act.copy(endT[:, :, :], end_ps[:, 0, 0:2 * P].rearrange("p (a n) -> p a n", a=2)).then_inc(e_Tc, 1)
                k = ends(i, 3)
                if k is not None and known(i, 3):
                    d = (i - 3) // G
                    over = act.value_load(longest_i[0:1, OVER, bass.ds(b + d, 1), k], min_val=0, max_val=2 * N // SLOTS)
                    with act.If(over > 0):
                        with act.Fori(0, over):
                            n = act.snap(seen)
                            act.wait_ge(o_prep, n + 1)
                            for j in range(SLOTS):
                                last = act.activation(o_squares[:, j, :], o_pre[:, j, :], ACT.Square, accum_out=o_ssq[:, j:j + 1])
                            last.then_inc(o_sums, 1)
                            act.wait_ge(o_root, n + 1)
                            for j in range(SLOTS):
                                last = act.activation(o_pre[:, j, :], o_pre[:, j, :], ACT.Identity, scale=o_rstd[:, j:j + 1])
                            last.then_inc(o_scaled, 1)
                            for half in range(2):
                                act.wait_ge(o_zt, 2 * n + half + 1)
                                act.activation(o_msgT[:, 4 * half:4 * half + 4, :], o_ps[:, 0, :].rearrange("p (s n) -> p s n", s=4),
                                               ACT.Gelu, bias=cols[:, 1:2], scale=cols[:, 0:1]).then_inc(o_gelu, 1)
                            act.reg_add(seen, seen, 1)

            chunk_loop(act, steps, G + 6, lead=7)

        @block.vector
        def _(dve):
            done = [0]

            def step(ins):
                done[0] += 1
                ins.then_inc(s_seq, 1)
                dve.wait_ge(s_seq, done[0])

            def rsqrt_step(j, v, ii, uu, y):
                if j == 0:
                    return dve.tensor_scalar(ii, v.bitcast(U32), 1, None, ALU.logical_shift_right)
                if j == 1:
                    return dve.tensor_scalar(y.bitcast(U32), ii, -1.0, MAGIC, ALU.mult, ALU.add)
                if j % 3 == 2:
                    return dve.scalar_tensor_tensor(uu, y, -0.5, y, ALU.mult, ALU.mult)
                if j % 3 == 0:
                    return dve.tensor_tensor(uu, uu, v, ALU.mult)
                return dve.scalar_tensor_tensor(y, uu, 1.5, y, ALU.add, ALU.mult)

            dve.wait_ge(s_const, 16 * N_CONST)
            dve.wait_ge(s_ident, 2)
            dve.wait_ge(s_iota, 4)
            for k in range(2):
                step(dve.reduce_sum(mean1[:, k:k + 1], w1_sb[:, k, :], AX.X))
            step(dve.reduce_sum(mean1[:, 2:3], b1_all, AX.X))
            step(dve.tensor_scalar(mean1[:, :], mean1[:, :], -1.0 / D, None, ALU.mult))
            for k in range(2):
                step(dve.tensor_scalar(w1_sb[:, k, :], w1_sb[:, k, :], mean1[:, k:k + 1], None, ALU.add))
            step(dve.tensor_scalar(b1_all, b1_all, mean1[:, 2:3], None, ALU.add))
            step(dve.tensor_scalar(cols[:, 0:1], cols[:, 0:1], ROOT_D, None, ALU.mult))
            step(dve.tensor_scalar(g2_all, g2_all, ROOT_D, None, ALU.mult))
            step(dve.tensor_copy(rest[:, :], b2_all))
            for k in range(3):
                step(dve.tensor_copy(parts[:, k, :], rest[:, :]))
                step(dve.tensor_tensor(rest[:, :], rest[:, :], parts[:, k, :], ALU.subtract))
            step(dve.tensor_scalar(b2_split[:, :], parts[0:3, 0, :], ident[0:3, 0:1], None, ALU.mult))
            for k in (1, 2):
                step(dve.scalar_tensor_tensor(b2_split[:, :], parts[0:3, k, :], ident[0:3, k:k + 1], b2_split[:, :], ALU.mult, ALU.add))
            step(dve.memset(ones3[:, :], 1.0))
            step(dve.memset(zeros[:, :], 0.0))
            step(dve.memset(nv[:, :], 1.0))
            dve.sem_inc(s_setup, 1)

            def graph(b, q, front, back):
                if front:
                    dve.wait_ge(g_load[q], 16 * b + (32 if q == 0 else 16))
                    if not (isinstance(b, int) and b == 0):
                        dve.wait_ge(g_ids, b)
                    for sign, op in enumerate((ALU.is_gt, ALU.is_lt)):
                        for it in range(TB):
                            last = dve.tensor_scalar(junk_v[:, sign, it, :], adj_g[:, q, it, :], 0.0, 0.0, op, ALU.add,
                                                     accum_out=count_g[:, sign, it:it + 1])
                    last.then_inc(g_count, 1)
                    dve.wait_ge(g_count, b + 1)
                    dve.scalar_tensor_tensor(sort_key[:, :], count_g[:, 0, :], float(N), backward[:, :], ALU.mult, ALU.add).then_inc(g_key, 1)
                if back:
                    dve.wait_ge(g_prod, b)
                    dve.wait_ge(g_xb, b)
                    for it in range(TB):
                        last = dve.scalar_tensor_tensor(pre_g[:, it, :], prod_ps[:, 0, it * D:(it + 1) * D], dis[:, it:it + 1],
                                                        xb_g[:, 1 - q, it, :], ALU.mult, ALU.add)
                    last.then_inc(g_pre, 1)
                    dve.wait_ge(g_pre, b)
                    for it in range(TB):
                        last = dve.bn_stats(stats_g[:, it, :], pre_g[:, it, :])
                    last.then_inc(g_stats, 1)
                    wait_alone(dve, g_stats, 2 * b - 1)
                    for it in range(TB):
                        last = dve.bn_aggr(mv_g[:, it, :], stats_g[:, it, :])
                    last.then_inc(g_stats, 1)
                    dve.wait_ge(g_stats, 2 * b)
                    last = dve.tensor_scalar(nv[:, TB:2 * TB], mv_g[:, :, 1], EPS, None, ALU.add)
                if front:
                    dve.wait_ge(g_deg, b + 1)
                    last = dve.tensor_scalar(nv[:, 0:TB], deg[:, :], 1.0, None, ALU.add)
                last.then_inc(g_nv, 1)
                dve.wait_ge(g_nv, b + 1)
                for j in range(STEPS):
                    if j:
                        dve.wait_ge(g_rs, b * STEPS + j)
                    rsqrt_step(j, nv[:, :], ni[:, :], nu[:, :], ny[:, :]).then_inc(g_rs, 1)
                dve.wait_ge(g_rs, (b + 1) * STEPS)
                if front:
                    dve.tensor_scalar(nonzero[:, :], nv[:, 0:TB], 0.0, None, ALU.not_equal).then_inc(g_mask, 1)
                if back:
                    if not (isinstance(b, int) and b < 3):
                        dve.wait_ge(g_store[1 - q], stored(b - 1, 1 - q))
                    for it in range(TB):
                        last = dve.tensor_scalar(own_g[:, 1 - q, it, 0:D], pre_g[:, it, :], mv_g[:, it, 0:1],
                                                 ny[:, TB + it:TB + it + 1], ALU.subtract, ALU.mult)
                    last.then_inc(g_h, 1)
                if front:
                    dve.wait_ge(g_mask, b + 1)
                    dve.tensor_tensor(dis[:, :], ny[:, 0:TB], nonzero[:, :], ALU.mult).then_inc(g_dis, 1)
                    dve.wait_ge(g_dis, b + 1)
                    if not (isinstance(b, int) and b == 0):
                        dve.wait_ge(g_prod, b)
                    dve.wait_ge(g_sup, b + 1)
                    dve.tensor_tensor(sup[:, :, :], sup_ps[:, 0, :].rearrange("p (t d) -> p t d", t=TB),
                                      dis[:, :].unsqueeze(2).to_broadcast([P, TB, D]), ALU.mult).then_inc(g_supc, 1)
                    for mt in range(2):
                        dve.wait_ge(g_adjT, 4 * b + mt + 3)
                        dve.tensor_copy(adjT[:, mt + 2, :], adjT2_ps[:, mt, :]).then_inc(g_adjTv, 1)
                    dve.wait_ge(g_keys, b + 1)
                    for it in range(TB):
                        last = dve.tensor_scalar(junk_v[:, 2, it, :], xT_ps[:, 0, :], sort_key[:, it:it + 1], 0.0, ALU.is_gt, ALU.add,
                                                 accum_out=rank[:, it:it + 1])
                    last.then_inc(g_rank, 1)
                    dve.wait_ge(g_rank, b + 1)
                    for it in range(TB):
                        last = dve.tensor_scalar(chosen[:, it, :], places[:, :], rank[:, it:it + 1], None, ALU.is_equal)
                    last.then_inc(g_chosen, 1)
                    for k in range(TB):
                        last = dve.scalar_tensor_tensor(reach[:, k, :], rank[:, :], float(k * P), count_g[:, 0, :], ALU.is_ge, ALU.mult)
                    last.then_inc(g_reach, 1)
                    dve.wait_ge(g_reach, b + 1)
                    at = bass.ds(b * TB, TB)
                    dve.tensor_reduce(counts[:, 0, at], reach[:, :, :], AX.X, ALU.max)
                    dve.tensor_reduce(counts[:, 1, at], count_g[:, 1, :].unsqueeze(1).to_broadcast([P, TB, TB]), AX.X, ALU.max)
                    dve.wait_ge(g_order, b + 1)
                    dve.tensor_scalar(row_id[:, at], hT_ps[:, 0, 0:TB], base[:, bass.ds(b * TB, 1)], None, ALU.add).then_inc(g_ids, 1)
                if back:
                    dve.wait_ge(g_m, b)
                    dve.tensor_tensor(own_g[:, 1 - q, :, D:2 * D], adjT_ps[:, 1, :].rearrange("p (t o) -> p t o", t=TB),
                                      b1_all.unsqueeze(1).to_broadcast([P, TB, D]), ALU.add).then_inc(g_mi, 1)

            graph_loop(dve, graph)

            dve.wait_ge(s_rows, 1)
            for sign in range(2):
                step(dve.reduce_max(most[:, sign:sign + 1], xT_ps[:, 0, sign * P:(sign + 1) * P], AX.X))
            dve.sem_inc(s_most, 1)
            dve.wait_ge(s_rows, 2)
            step(dve.tensor_copy(longest_f[:, :, :, :], sup_ps[0:1, 0, 0:2 * TILES].rearrange("p (s b k) -> p s b k", s=2, k=TB)))
            step(dve.tensor_copy(longest_i[:, LONGEST, :, :], longest_f[:, 0, :, :]))
            for k in range(TB):
                most_slots = CHUNKS[k] * SLOTS
                step(dve.tensor_scalar(longest_i[:, OVER_POS, :, k], longest_f[:, 0, :, k], float(most_slots),
                                       float(SLOTS - 1 - most_slots), ALU.max, ALU.add))
            step(dve.tensor_scalar(longest_i[:, OVER_NEG, :, :], longest_f[:, 1, :, :], float(SLOTS - 1), None, ALU.add))
            for k in (OVER_POS, OVER_NEG):
                step(dve.tensor_scalar(longest_i[:, k, :, :], longest_i[:, k, :, :], 3, None, ALU.logical_shift_right))
            step(dve.tensor_tensor(longest_i[:, OVER, :, :], longest_i[:, OVER_POS, :, :], longest_i[:, OVER_NEG, :, :], ALU.add))
            for m, (k, c) in enumerate(MAYBE):
                step(dve.tensor_scalar(sized[:, :], longest_f[:, 0, :, k], float(-c * SLOTS), 0.0, ALU.add, ALU.max))
                step(dve.tensor_scalar(sized[:, :], sized[:, :], float(SLOTS), 16.0, ALU.min, ALU.mult))
                step(dve.tensor_tensor_scan(summed[:, :], sized[:, :], zeros[:, :], 0.0, ALU.add, ALU.add))
                step(dve.tensor_copy(arrivals[:, m, :], summed[:, :]))
            dve.sem_inc(s_ready, 1)
            dve.wait_ge(s_zero, 2)

            seen = dve.alloc_register("dve_overflow_seen")
            dve.reg_mov(seen, 0)

            def steps(b, bG, i, known):
                if known(i):
                    k, c = tile_of(i)
                    if c == 0:
                        dve.wait_ge(t_own[k], 16 * (b + 1))
                    if (k, c) not in MAYBE:
                        r = i % RING
                        others = [j for j in range(G) if j % RING == r and tile_of(j) not in MAYBE]
                        dve.wait_ge(t_rows[r], (b * len(others) + others.index(i) + 1) * (16 * SLOTS))
                    else:
                        longest = dve.value_load(longest_i[0:1, LONGEST, bass.ds(b, 1), k], min_val=0, max_val=N)
                        with dve.If(longest > c * SLOTS):
                            m = MAYBE.index((k, c))
                            value = dve.value_load(arrivals[0:1, m, bass.ds(b, 1)], min_val=16, max_val=16 * SLOTS * B)
                            wait_alone(dve, t_maybe[m], value)
                    if known(i, RG):
                        dve.wait_ge(t_zt, bG + i - RG + 1)
                    dve.tensor_tensor(pre[:, i % RG, :, :], gathered[:, i % RING * SLOTS:(i % RING + 1) * SLOTS, :],
                                      own_t[:, k, D:2 * D].unsqueeze(1).to_broadcast([P, SLOTS, D]), ALU.add).then_inc(t_pre, 1)
                k1 = ends(i, 7) if known(i, 7) else None
                k2 = ends(i, 8) if known(i, 8) else None
                def link(e, ins, n):
                    ins.then_inc(e_seq, 1)
                    dve.wait_ge(e_seq, e * E_STEPS + n)
                if k1 is not None:
                    e = tiles_before(b, i, 7)
                    dve.wait_ge(e_upd, e + 1)
                    link(e, dve.bn_stats(stats[:, :], end_ps[:, 0, 2 * P:3 * P]), 1)
                    dve.sem_inc(s_carrier[dve.engine], 1)
                    link(e, dve.bn_aggr(mv[:, :], stats[:, :]), 2)
                    link(e, dve.tensor_scalar(ssq[:, (i - 1) % RG, SLOTS:], mv[:, 1:2], float(D), None, ALU.mult), 3)
                if known(i, -AHEAD):
                    s, sk = bG + i + AHEAD, tile_of(i + AHEAD)[0]
                    si = (i + AHEAD) % G
                    if begins(i, -AHEAD) is not None:
                        wait_alone(dve, t_key, tiles_before(b, i, -AHEAD) + 1)
                    else:
                        wait_alone(dve, t_zap, s)
                    dve.max(weight[:, si, :], key[:, sk, :]).then_inc(t_max, 1)
                if known(i, 1) or i > G:
                    r = (i - 1) % RG
                    if known(i, 1):
                        dve.wait_ge(t_ssq, bG + i)
                    if k1 is not None:
                        dve.wait_ge(e_seq, e * E_STEPS + 3)
                    if k2 is not None:
                        dve.wait_ge(e_var, tiles_before(b, i, 8) + 1)
                    dve.tensor_scalar(rs_v[:, :], ssq[:, r, :], D * EPS, None, ALU.add).then_inc(t_rs, 1)
                    for j in range(STEPS):
                        dve.wait_ge(t_rs, (bG + i - 1) * (STEPS + 1) + j + 1)
                        rsqrt_step(j, rs_v[:, :], rs_i[:, :], rs_u[:, :], rstd[:, r, :]).then_inc(t_rs, 1)
                if known(i, -AHEAD):
                    wait_alone(dve, t_max, s + 1)
                    dve.max_index(found[:, si, :], weight[:, si, :], key[:, sk, :]).then_inc(t_find, 1)
                    dve.match_replace(out=key[:, sk, :], in_to_replace=weight[:, si, :], in_values=key[:, sk, :],
                                      imm_value=0.0).then_inc(t_zap, 1)
                    dve.wait_ge(t_find, s + 1)
                    first_row = base[:, bass.ds(tiles_before(b, i, -AHEAD), 1)]
                    dve.tensor_scalar(index[:, si, :], found[:, si, :], first_row, None, ALU.add).then_inc(t_idx, 1)
                if k1 is not None:
                    dve.wait_ge(t_rs, (bG + i) * (STEPS + 1))
                    link(e, dve.tensor_scalar(upd[:, :], end_ps[:, 0, 2 * P:3 * P], mv[:, 0:1], rstd[:, (i - 1) % RG, SLOTS:],
                                              ALU.subtract, ALU.mult), 4)
                    link(e, dve.tensor_tensor(upd[:, :], upd[:, :], g2_all, ALU.mult), 5)
                    link(e, dve.tensor_tensor(res[:, :], own_t[:, k1, 0:D], be2_all, ALU.add), 6)
                    link(e, dve.tensor_tensor(res[:, :], res[:, :], upd[:, :], ALU.add), 7)
                    link(e, dve.bn_stats(stats[:, :], res[:, :]), 8)
                    dve.sem_inc(s_carrier[dve.engine], 1)
                    link(e, dve.bn_aggr(mv[:, :], stats[:, :]), 9)
                    dve.tensor_scalar(ssq[:, i % RG, SLOTS:], mv[:, 1:2], float(D), None, ALU.mult).then_inc(e_var, 1)
                if k2 is not None:
                    e = tiles_before(b, i, 8)
                    dve.wait_ge(t_rs, (bG + i) * (STEPS + 1))
                    dve.tensor_scalar(r_end[:, :], rstd[:, (i - 1) % RG, SLOTS:], ROOT_D, None, ALU.mult).then_inc(e_root, 1)
                    dve.wait_ge(e_root, e + 1)
                    if not (isinstance(e, int) and e < 2):
                        dve.wait_ge(e_store[k2 % 2], 8 * (e - k2 % 2))
                    dve.tensor_scalar(out_sb[:, k2 % 2, :], res[:, :], mv[:, 0:1], r_end[:, :], ALU.subtract, ALU.mult).then_inc(e_out, 1)
                if known(i, 3):
                    dve.wait_ge(t_zb, bG + i - 2)
                    if known(i, 3 + RG):
                        dve.wait_ge(t_agg, bG + i - 2 - RG)
                    dve.tensor_tensor(msg[:, i % RG, :, :], zb_ps[:, :, :].rearrange("p h (s o) -> p (h s) o", s=4),
                                      weight[:, (i - 3) % G, :].unsqueeze(2).to_broadcast([P, SLOTS, D]), ALU.mult).then_inc(t_wmsg, 1)
                k = ends(i, 3)
                if k is not None and known(i, 3):
                    g = b + (i - 3) // G
                    wait_alone(dve, t_wmsg, bG + i - 2)
                    over = dve.value_load(longest_i[0:1, OVER_POS, bass.ds(g, 1), k], min_val=0, max_val=N // SLOTS)
                    with dve.If(over > 0):
                        with dve.Fori(0, over):
                            overflow_chunk(g, k, 1.0)
                    over = dve.value_load(longest_i[0:1, OVER_NEG, bass.ds(g, 1), k], min_val=0, max_val=N // SLOTS)
                    with dve.If(over > 0):
                        dve.tensor_scalar(key[:, k, :], adj_t[:, k, :], -1.0, 0.0, ALU.mult, ALU.max).then_inc(o_key, 1)
                        dve.wait_ge(o_key, 1)
                        dve.sem_clear(o_key)
                        with dve.Fori(0, over):
                            overflow_chunk(g, k, -1.0)
                    dve.sem_inc(t_over, 1)

            O_STEPS = 6 + STEPS

            def overflow_chunk(g, k, sign):
                n = dve.snap(seen)
                count = [0]
                def link(ins):
                    count[0] += 1
                    ins.then_inc(o_seq, 1)
                    wait_alone(dve, o_seq, n * O_STEPS + count[0])
                link(dve.max(o_weight[:, :], key[:, k, :]))
                link(dve.max_index(o_found[:, :], o_weight[:, :], key[:, k, :]))
                link(dve.match_replace(out=key[:, k, :], in_to_replace=o_weight[:, :], in_values=key[:, k, :], imm_value=0.0))
                link(dve.tensor_scalar(o_weight[:, :], o_weight[:, :], sign, None, ALU.mult))
                dve.tensor_scalar(o_index[:, :], o_found[:, :], base[:, bass.ds(g * TB, 1)], None, ALU.add).then_inc(o_idx, 1)
                dve.wait_ge(o_rows, n + 1)
                link(dve.tensor_tensor(o_pre[:, :, :], o_pre[:, :, :], own_t[:, k, D:2 * D].unsqueeze(1).to_broadcast([P, SLOTS, D]), ALU.add))
                dve.sem_inc(o_prep, 1)
                dve.wait_ge(o_sums, n + 1)
                link(dve.tensor_scalar(o_ssq[:, :], o_ssq[:, :], D * EPS, None, ALU.add))
                for j in range(STEPS):
                    link(rsqrt_step(j, o_ssq[:, :], rs_i[:, 0:SLOTS], rs_u[:, 0:SLOTS], o_rstd[:, :]))
                dve.sem_inc(o_root, 1)
                for half in range(2):
                    dve.wait_ge(o_zb, 2 * n + half + 1)
                    at = slice(4 * half, 4 * half + 4)
                    dve.tensor_tensor(o_msg[:, at, :], o_ps[:, 0, :].rearrange("p (s o) -> p s o", s=4),
                                      o_weight[:, at].unsqueeze(2).to_broadcast([P, 4, D]), ALU.mult).then_inc(o_wmsg, 1)
                dve.wait_ge(o_agg, n + 1)
                dve.reg_add(seen, seen, 1)

            chunk_loop(dve, steps, G + 8, lead=AHEAD)

        @block.tensor
        def _(pe):
            pe.wait_ge(s_ident, 2)
            pe.wait_ge(s_setup, 1)
            mm, transpose = nc.tensor.matmul, nc.tensor.transpose

            def graph(b, q, front, back):
                first = isinstance(b, int) and b == 0
                if back:
                    pe.wait_ge(g_supc, b)
                    pe.wait_ge(g_adjTa, 2 * b)
                    pe.wait_ge(g_adjTv, 2 * b)
                    if not (isinstance(b, int) and b == 1):
                        pe.wait_ge(g_pre, b - 1)
                    for it in range(TB):
                        dst = prod_ps[:, 0, it * D:(it + 1) * D]
                        for mt in range(TB):
                            mm(dst, adjT[:, mt, it * P:(it + 1) * P], sup[:, mt, :], start=(mt == 0), stop=False)
                        last = mm(dst, ident[:, :], sup[:, it, :], start=False, stop=True)
                    last.then_inc(g_prod, 1)
                if front:
                    pe.wait_ge(g_load[q], 16 * b + (32 if q == 0 else 16))
                    if not first:
                        pe.wait_ge(g_rank, b)
                    for it in range(TB):
                        last = transpose(xT_ps[:, 0, it * P:(it + 1) * P], x_g[:, q, it, :], ident[:, :])
                    last.then_inc(g_xT, 1)
                    if not (isinstance(b, int) and b < 2):
                        pe.wait_ge(g_mj, b - 1)
                        pe.wait_ge(g_mi, b - 1)
                    for mt in range(TB):
                        dst = (adjT_ps, adjT2_ps)[mt // 2]
                        for it in range(TB):
                            last = transpose(dst[:, mt % 2, it * P:(it + 1) * P], adj_g[:, q, it, mt * P:(mt + 1) * P], ident[:, :])
                        last.then_inc(g_adjT, 1)
                if back:
                    pe.wait_ge(g_h, b)
                    pe.wait_ge(g_ids, b)
                    for it in range(TB):
                        last = transpose(hT_ps[:, 0, it * P:(it + 1) * P], own_g[:, 1 - q, it, 0:D], ident[:, :])
                    last.then_inc(g_hT, 1)
                if front:
                    pe.wait_ge(g_xTc, b + 1)
                    if not first:
                        pe.wait_ge(g_supc, b)
                    for it in range(TB):
                        last = mm(sup_ps[:, 0, it * D:(it + 1) * D], xT[:, it * P:(it + 1) * P], w0_sb[:, :], start=True, stop=True)
                    last.then_inc(g_sup, 1)
                    pe.wait_ge(g_key, b + 1)
                    for it in range(TB):
                        last = mm(xT_ps[:, 0, it * P:(it + 1) * P], sort_key[:, it:it + 1].to_broadcast([P, P]), ident[:, :],
                                  start=True, stop=True)
                    last.then_inc(g_keys, 1)
                if back:
                    pe.wait_ge(g_hTc, b)
                    if front:
                        pe.wait_ge(g_adjTa, 2 * b + 2)
                    for k in range(2):
                        for it in range(TB):
                            last = mm(adjT_ps[:, k, it * D:(it + 1) * D], hT[:, it * P:(it + 1) * P], w1_sb[:, k, :], start=True, stop=True)
                    last.then_inc(g_m, 1)
                if front:
                    pe.wait_ge(g_chosen, b + 1)
                    for k in range(TB):
                        for it in range(TB):
                            last = mm(hT_ps[:, 0, k:k + 1], chosen[:, it, k * P:(k + 1) * P], number[:, it:it + 1],
                                      start=(it == 0), stop=(it == TB - 1))
                    last.then_inc(g_order, 1)

            graph_loop(pe, graph)

            pe.wait_ge(g_ids, B)
            pe.wait_ge(g_supc, B)
            for sign in range(2):
                last = transpose(xT_ps[:, 0, sign * P:(sign + 1) * P], counts[:, sign, :], ident[:, :])
            last.then_inc(s_rows, 1)
            pe.wait_ge(s_most, 1)
            for sign in range(2):
                last = mm(sup_ps[0:1, 0, sign * P:(sign + 1) * P], most[:, sign:sign + 1], ident[:, :], start=True, stop=True)
            last.then_inc(s_rows, 1)
            pe.wait_ge(s_ready, 1)
            pe.wait_ge(g_mi, B)
            pe.wait_ge(g_mj, B)

            seen = pe.alloc_register("pe_overflow_seen")
            pe.reg_mov(seen, 0)

            def steps(b, bG, i, known):
                k = ends(i, 6)
                if k is not None and known(i, 6):
                    pe.wait_ge(e_Tc, tiles_before(b, i, 6) + 1)
                    u = end_ps[:, 0, 2 * P:3 * P]
                    mm(u, endT[:, 1, :], w2_sb[:, 0, :], start=True, stop=False)
                    mm(u, endT[:, 0, :], w2_sb[:, 1, :], start=False, stop=False)
                    mm(u, ones3[:, :], b2_split[:, :], start=False, stop=True).then_inc(e_upd, 1)
                if known(i, 1):
                    pe.wait_ge(t_scaled, bG + i)
                    if known(i, 2):
                        pe.wait_ge(t_gelu, bG + i - 1)
                    for j in range(SLOTS):
                        last = transpose(zt_ps[:, j // 4, j % 4 * P:(j % 4 + 1) * P], pre[:, (i - 1) % RG, j, :], ident[:, :])
                    last.then_inc(t_zt, 1)
                if known(i, 2):
                    pe.wait_ge(t_gelu, bG + i - 1)
                    if known(i, 3):
                        pe.wait_ge(t_wmsg, bG + i - 2)
                    for j in range(SLOTS):
                        last = transpose(zb_ps[:, j // 4, j % 4 * D:(j % 4 + 1) * D], msgT[:, (i - 2) % RG, j, :], ident[:, :])
                    last.then_inc(t_zb, 1)
                if known(i, 3):
                    k, c = tile_of(i - 3)
                    t = tiles_before(b, i, 3)
                    pe.wait_ge(t_wmsg, bG + i - 2)
                    if c == 0 and not (isinstance(t, int) and t < 2):
                        pe.wait_ge(e_agg, t - 1)
                    for half in range(2):
                        last = mm(agg_ps[k % 2][:, 0, :], ident[:, :], msg[:, i % RG, 4 * half:4 * half + 4, :].rearrange("p s o -> p (s o)"),
                                  start=(c == 0 and half == 0), stop=True, skip_group_check=True)
                    last.then_inc(t_agg, 1)
                k = ends(i, 4)
                if k is not None and known(i, 4):
                    t = tiles_before(b, i, 4)
                    pe.wait_ge(e_agg, t + 1)
                    if not (isinstance(t, int) and t == 0):
                        pe.wait_ge(e_seq, (t - 1) * E_STEPS + 4)
                    for s4 in range(4):
                        mm(end_ps[:, 0, 0:P], agg_sb[:, s4, :], ident[:, :], start=(s4 == 0), stop=(s4 == 3))
                    transpose(end_ps[:, 0, P:2 * P], own_t[:, k, 0:D], ident[:, :]).then_inc(e_T, 1)
                k = ends(i, 3)
                if k is not None and known(i, 3):
                    d = (i - 3) // G
                    over = pe.value_load(longest_i[0:1, OVER, bass.ds(b + d, 1), k], min_val=0, max_val=2 * N // SLOTS)
                    with pe.If(over > 0):
                        with pe.Fori(0, over):
                            n = pe.snap(seen)
                            pe.wait_ge(o_scaled, n + 1)
                            for half in range(2):
                                if half:
                                    pe.wait_ge(o_wmsg, 2 * n + 1)
                                for j in range(4):
                                    last = transpose(o_ps[:, 0, j * P:(j + 1) * P], o_pre[:, 4 * half + j, :], ident[:, :])
                                last.then_inc(o_zt, 1)
                                pe.wait_ge(o_gelu, 2 * n + half + 1)
                                for j in range(4):
                                    last = transpose(o_ps[:, 0, j * D:(j + 1) * D], o_msgT[:, 4 * half + j, :], ident[:, :])
                                last.then_inc(o_zb, 1)
                            pe.wait_ge(o_wmsg, 2 * n + 2)
                            for half in range(2):
                                last = mm(agg_ps[k % 2][:, 0, :], ident[:, :], o_msg[:, 4 * half:4 * half + 4, :].rearrange("p s o -> p (s o)"),
                                          start=False, stop=True, skip_group_check=True)
                            last.then_inc(o_agg, 1)
                            pe.wait_ge(o_agg, n + 1)
                            pe.reg_add(seen, seen, 1)
                    pe.wait_ge(t_agg, bG + i - 2)
                    pe.sem_inc(t_sum, 1)

            chunk_loop(pe, steps, G + 6)


INS = ["x", "adj", "L0_gnn_weight", "L0_gnn_bias", "L1_gnn_W1", "L1_gnn_b1", "L1_gnn_g1", "L1_gnn_be1",
       "L1_gnn_W2", "L1_gnn_b2", "L1_gnn_g2", "L1_gnn_be2"]


def kernel(**inputs):
    import concourse.bacc as bacc
    from concourse.bass_utils import run_bass_kernel_spmd

    nc = bacc.Bacc("TRN2", target_bir_lowering=False, num_devices=1)
    arrays = {f"in_{n}": np.ascontiguousarray(inputs[n]) for n in INS}
    args = [nc.dram_tensor(n, a.shape, mybir.dt.from_np(a.dtype), kind="ExternalInput").ap() for n, a in arrays.items()]
    out = nc.dram_tensor("out_0", (B, N, D), FP32, kind="ExternalOutput").ap()
    adj_resnorm_kernel(nc, *args, out)
    r = run_bass_kernel_spmd(nc, [arrays], core_ids=[0])
    return r.results[0]["out_0"]
```

```python
from contextlib import ExitStack

import numpy as np
import concourse.bass as bass
from concourse import mybir

FP32 = mybir.dt.float32
BF16 = mybir.dt.bfloat16
U32 = mybir.dt.uint32
I32 = mybir.dt.int32
ALU = mybir.AluOpType
ACT = mybir.ActivationFunctionType
AX = mybir.AxisListType

B, N, D = 32, 512, 128
P = 128
TB = N // P
TILES = B * TB
SLOTS = 8
CHUNKS = (7, 5, 5, 4)
STARTS = (0, 7, 12, 17)
G = sum(CHUNKS)
MAYBE = ((0, 5), (0, 6), (1, 4), (2, 3), (2, 4), (3, 3))
AHEAD = 6
RING = 7
RG = 3
EPS = 1e-5
MAGIC = float(0x5F3759DF)
STEPS = 11
ROOT_D = float(np.float32(np.sqrt(D)))


def tile_of(i):
    j = i % G
    k = max(k for k in range(TB) if STARTS[k] <= j)
    return k, j - STARTS[k]


def adj_resnorm_kernel(nc, x, adj, w0, b0, w1, b1, g1, be1, w2, b2, g2, be2, out):
    x_rows = x.rearrange("b (t p) d -> b p t d", p=P)
    adj_rows = adj.rearrange("b (t p) m -> b p t m", p=P)
    adj_flat = adj.rearrange("b n m -> (b n) m")
    out_flat = out.rearrange("b n d -> (b n) d")

    ctx = ExitStack()
    with ctx:
        def sb(name, shape, dt=FP32):
            return ctx.enter_context(nc.sbuf_tensor(name, shape, dt))

        def sem(name):
            return ctx.enter_context(nc.semaphore(name))

        msg_j = nc.dram_tensor("msg_j", [B * N, D], FP32).ap()
        own = nc.dram_tensor("own", [B * N, 2 * D], FP32).ap()

        ident = sb("ident", [P, P])
        w0_sb = sb("w0_sb", [P, D])
        w1_sb = sb("w1_sb", [P, 2, D])
        w2_sb = sb("w2_sb", [P, 2, D])
        vecs = sb("vecs", [P, 5, D])
        b0_all, b1_all, b2_all, g2_all, be2_all = (vecs[:, k, :] for k in range(5))
        cols = sb("cols", [P, 2])
        mean1 = sb("mean1", [P, 3])
        parts = sb("parts", [P, 3, D], BF16)
        rest = sb("rest", [P, D])
        b2_split = sb("b2_split", [3, D], BF16)
        ones3 = sb("ones3", [3, P], BF16)
        base = sb("base", [P, TILES])
        number = sb("number", [P, TB])
        backward = sb("backward", [P, TB])
        places = sb("places", [P, N])

        adj_g = sb("adj_g", [P, TB, N])
        x_g = sb("x_g", [P, TB, D])
        xb_g = sb("xb_g", [P, TB, D])
        xT = sb("xT", [P, N])
        deg = sb("deg", [P, TB])
        nonzero = sb("nonzero", [P, TB])
        dis = sb("dis", [P, TB])
        sup = sb("sup", [P, TB, D])
        adjT = sb("adjT", [P, TB, N])
        pre_g = sb("pre_g", [P, TB, D])
        stats_g = sb("stats_g", [P, TB, 6])
        mv_g = sb("mv_g", [P, TB, 2])
        own_g = sb("own_g", [P, TB, 2 * D])
        hT = sb("hT", [P, N])
        mj_g = sb("mj_g", [P, TB, D])
        junk_a = sb("junk_a", [P, TB, N], BF16)
        junk_v = sb("junk_v", [P, 3, TB, N], BF16)
        facts = sb("facts", [P, TB, 2])
        negative = sb("negative", [P, TB])
        ones = sb("ones", [P, P])
        sort_key = sb("sort_key", [P, TB])
        rank = sb("rank", [P, TB])
        chosen = sb("chosen", [P, TB, N])
        row_id = sb("row_id", [P, TILES], U32)
        longest_f = sb("longest_f", [1, TB])
        pos_f = sb("pos_f", [1, TB])
        neg_f = sb("neg_f", [1, 1])
        whole = sb("whole", [1, 2, TB])
        sized = sb("sized", [1, len(MAYBE)])
        summed = sb("summed", [1, len(MAYBE)])
        over_i = sb("over_i", [1, 3, TB], I32)
        zeros = sb("zeros", [P, 16 * D])
        longest_i = sb("longest_i", [1, 4, B, TB], I32)
        LONGEST, OVER_POS, OVER_NEG, OVER = range(4)
        arrivals = sb("arrivals", [1, len(MAYBE), B], I32)

        adj_t = sb("adj_t", [P, TB, N])
        key = sb("key", [P, TB, N])
        ids_adj = sb("ids_adj", [P, TB], U32)
        ids_row = sb("ids_row", [P, TB], U32)
        own_t = sb("own_t", [P, TB, 2 * D])
        weight = sb("weight", [P, G, SLOTS])
        found = sb("found", [P, G, SLOTS], U32)
        index = sb("index", [P, G, SLOTS], U32)
        gathered = sb("gathered", [P, RING * SLOTS, D])
        pre = sb("pre", [P, RG, SLOTS, D])
        squares = sb("squares", [P, RG, SLOTS, D], BF16)
        ssq = sb("ssq", [P, RG, SLOTS + 1])
        DEG, VAR, ROOTS = SLOTS + 1, SLOTS + 1 + TB, SLOTS + 1 + 2 * TB
        rstd = sb("rstd", [P, RG, ROOTS])
        rs_v = sb("rs_v", [P, ROOTS])
        rs_i = sb("rs_i", [P, ROOTS], U32)
        rs_u = sb("rs_u", [P, ROOTS])
        msgT = sb("msgT", [P, RG, SLOTS, P])
        msg = sb("msg", [P, RG, SLOTS, D])
        agg_sb = sb("agg_sb", [P, 4, D])
        endT = sb("endT", [P, 2, P])
        upd = sb("upd", [P, D])
        res = sb("res", [P, D])
        stats = sb("stats", [P, 6])
        mv = sb("mv", [P, 2])
        r_end = sb("r_end", [P, 1])
        out_sb = sb("out_sb", [P, 2, D])
        o_weight = sb("o_weight", [P, SLOTS])
        o_found = sb("o_found", [P, SLOTS], U32)
        o_index = sb("o_index", [P, SLOTS], U32)
        o_pre = sb("o_pre", [P, SLOTS, D])
        o_squares = sb("o_squares", [P, SLOTS, D], BF16)
        o_ssq = sb("o_ssq", [P, SLOTS])
        o_rstd = sb("o_rstd", [P, SLOTS])
        o_msgT = sb("o_msgT", [P, SLOTS, P])
        o_msg = sb("o_msg", [P, SLOTS, D])

        def pb(name, banks):
            return ctx.enter_context(nc.psum_tensor(name, [P, banks, 512], FP32))
        agg_ps = (pb("agg_even_ps", 1), pb("agg_odd_ps", 1))
        end_ps = pb("end_ps", 1)
        o_ps = pb("o_ps", 1)
        zt_ps = pb("zt_ps", 2)
        zb_ps = pb("zb_ps", 2)

        s_const, s_ident, s_iota, s_zero, s_seq, s_setup = (
            sem(f"s_{n}") for n in ("const", "ident", "iota", "zero", "seq", "setup"))
        (g_load, g_store, g_xb, g_xT, g_xTc, g_deg, g_count, g_key, g_keys, g_nv, g_rs, g_mask, g_dis, g_sup, g_supc,
         g_adjT, g_adjTc, g_prod, g_pre, g_stats, g_h, g_hT, g_hTc, g_m, g_mj, g_mi, g_rank, g_chosen, g_order, g_ids,
         g_table, g_listed, g_zeros) = (
            sem(f"g_{n}") for n in ("load", "store", "xb", "xT", "xTc", "deg", "count", "key", "keys", "nv", "rs", "mask",
                                    "dis", "sup", "supc", "adjT", "adjTc", "prod", "pre", "stats", "h", "hT", "hTc", "m",
                                    "mj", "mi", "rank", "chosen", "order", "ids", "table", "listed",
                                    "zeros"))
        t_adj = [sem(f"t_adj{k}") for k in range(TB)]
        t_own = [sem(f"t_own{k}") for k in range(TB)]
        t_rows = [sem(f"t_rows{r}") for r in range(RING)]
        t_maybe = [sem(f"t_maybe{m}") for m in range(len(MAYBE))]
        t_ids_adj, t_ids_row = sem("t_ids_adj"), sem("t_ids_row")
        (t_key, t_max, t_find, t_zap, t_idx, t_pre, t_ssq, t_rs, t_scaled, t_zt, t_gelu, t_zb, t_wmsg, t_agg, t_over,
         t_sum) = (sem(f"t_{n}") for n in ("key", "max", "find", "zap", "idx", "pre", "ssq", "rs", "scaled", "zt", "gelu",
                                           "zb", "wmsg", "agg", "over", "sum"))
        e_agg, e_T, e_Tc, e_upd, e_seq, e_var, e_root, e_out = (
            sem(f"e_{n}") for n in ("agg", "T", "Tc", "upd", "seq", "var", "root", "out"))
        e_store = [sem(f"e_store{q}") for q in range(2)]
        o_key, o_seq, o_idx, o_dma, o_rows, o_prep, o_sums, o_root, o_scaled, o_zt, o_gelu, o_zb, o_wmsg, o_agg = (
            sem(f"o_{n}") for n in ("key", "seq", "idx", "dma", "rows", "prep", "sums", "root", "scaled", "zt", "gelu",
                                    "zb", "wmsg", "agg"))
        s_carrier = {e.engine: sem(f"s_carrier{k}") for k, e in enumerate((nc.sync, nc.gpsimd, nc.vector, nc.tensor))}

        block = ctx.enter_context(nc.Block())
        N_CONST = 3 + 5 + 2
        E_STEPS = 9

        def wait_alone(eng, sem, value):
            eng.wait_ge(sem, value)
            eng.sem_inc(s_carrier[eng.engine], 1)

        def prepare_first(piece):
            for a in range(2):
                for i in range(G):
                    piece(a, i, True)

        def chunk_loop(eng, steps, until, lead=0):
            def graph(b, first, last, prepares):
                def known(i, off=0):
                    return not (first and i - off < 0) and not (last and i - off >= G)
                bG, a = (b * G, b + 2) if isinstance(b, int) else (eng.snap(b * G), eng.snap(b + 2))
                for i in range(-lead if first else 0, until if last else G):
                    steps(b, a if prepares and i >= 0 else None, bG, i, known)
            graph(0, True, False, True)
            with eng.Fori(1, B - 2) as b:
                graph(b, False, False, True)
            graph(B - 2, False, False, False)
            graph(B - 1, False, True, False)

        def ends(i, off):
            k, c = tile_of(i - off)
            return k if c == CHUNKS[k] - 1 else None

        def begins(i, off):
            k, c = tile_of(i - off)
            return k if c == 0 else None

        def graph_of(b, i, off):
            return b + (i - off) // G

        def tiles_before(b, i, off):
            return b * TB + (i - off) // G * TB + tile_of(i - off)[0]

        @block.sync
        def _(sp):
            sp.dma_start(w0_sb[:, :], w0).then_inc(s_const, 16)
            sp.dma_start(w1_sb[:, :, :], w1.rearrange("(k p) o -> p k o", p=P)).then_inc(s_const, 16)
            sp.dma_start(w2_sb[:, :, :], w2.rearrange("(k p) o -> p k o", p=P)).then_inc(s_const, 16)
            for k, v in enumerate((b0, b1, b2, g2, be2)):
                sp.dma_start(vecs[:, k, :], v.rearrange("(a n) -> a n", a=1).partition_broadcast(P)).then_inc(s_const, 16)
            for k, v in enumerate((g1, be1)):
                sp.dma_start(cols[:, k:k + 1], v.rearrange("(n a) -> n a", a=1)).then_inc(s_const, 16)

            def load(a):
                if not (isinstance(a, int) and a == 0):
                    wait_alone(sp, g_xb, a)
                    wait_alone(sp, g_xT, a)
                    wait_alone(sp, g_adjT, a * 4)
                    wait_alone(sp, g_deg, a)
                    wait_alone(sp, g_count, a * 2)
                sp.dma_start(x_g[:, :, :], x_rows[a]).then_inc(g_load, 16)
                sp.dma_start(adj_g[:, :, :], adj_rows[a]).then_inc(g_load, 16)

            def store(a):
                wait_alone(sp, g_mj, a + 1)
                wait_alone(sp, g_mi, a + 1)
                rows = bass.ds(a * N, N)
                sp.dma_start(msg_j[rows, :].rearrange("(t p) d -> p t d", p=P), mj_g[:, :, :]).then_inc(g_store, 16)
                sp.dma_start(own[rows, :].rearrange("(t p) d -> p t d", p=P), own_g[:, :, :]).then_inc(g_store, 16)

            load(0)
            sp.wait_ge(s_zero, 1)
            for tensor, width in ((msg_j, D), (own, 2 * D)):
                times = B * N * width // (P * 16 * D)
                sp.dma_start(tensor.rearrange("(p n) d -> p (n d)", p=P).rearrange("p (k w) -> p k w", k=times),
                             zeros[:, :].unsqueeze(1).to_broadcast([P, times, 16 * D])).then_inc(g_zeros, 16)
            sp.wait_ge(g_zeros, 32)
            with sp.Fori(0, B - 1) as a:
                load(a + 1)
                store(a)
            store(B - 1)
            sp.wait_ge(g_store, 32 * B)

        @block.gpsimd
        def _(pool):
            pool.memset(zeros[:, :], 0.0).then_inc(s_zero, 1)
            pool.memset(ident[:, :], 0.0).then_inc(s_ident, 1)
            pool.wait_ge(s_ident, 1)
            pool.affine_select(out=ident[:, :], in_=ident[:, :], compare_op=ALU.not_equal, fill=1.0,
                               base=0, pattern=[[-1, P]], channel_multiplier=1).then_inc(s_ident, 1)
            for tensor, pattern, start, step in ((base, [[N, B], [0, TB]], 0, 0), (number, [[P, TB]], 0, 1),
                                                 (backward, [[-P, TB]], N - 1, -1), (places, [[1, N]], 0, 0)):
                pool.iota(tensor[:, :], pattern, base=start, channel_multiplier=step,
                          allow_small_or_imprecise_dtypes=True).then_inc(s_iota, 1)
            pool.memset(gathered[:, :, :], 0.0).then_inc(s_zero, 1)
            pool.memset(ssq[:, :, :], 1.0).then_inc(s_zero, 1)
            pool.wait_ge(s_zero, 3)

            seen = pool.alloc_register("pool_overflow_seen")
            pool.reg_mov(seen, 0)

            def rows_of(source, into, idx, done):
                pool.indirect_dma_start(into, None, source, bass.IndirectOffsetOnAxis(ap=idx, axis=0)).then_inc(done, 16)

            def copy_ids(into, t, k, copied):
                pool.tensor_copy(into[:, k:k + 1], row_id[:, bass.ds(t, 1)]).then_inc(copied, 1)
                wait_alone(pool, copied, t + 1)
                return into[:, k:k + 1]

            def adj_of(b, i, off):
                t, k = tiles_before(b, i, off), tile_of(i - off)[0]
                if k == 0:
                    wait_alone(pool, g_ids, graph_of(b, i, off) + 1)
                if not (isinstance(t, int) and t < TB):
                    wait_alone(pool, t_adj[k], 16 * graph_of(b, i, off))
                    wait_alone(pool, t_over, t - TB + 1)
                rows_of(adj_flat, adj_t[:, k, :], copy_ids(ids_adj, t, k, t_ids_adj), t_adj[k])

            def own_of(b, i, off):
                t, k = tiles_before(b, i, off), tile_of(i - off)[0]
                if k == 0:
                    wait_alone(pool, g_store, (graph_of(b, i, off) + 1) * 32)
                if not (isinstance(t, int) and t < TB):
                    wait_alone(pool, e_out, t - TB + 1)
                    wait_alone(pool, e_store[k % 2], 8 * (t - k % 2) - 16)
                rows_of(own, own_t[:, k, :], copy_ids(ids_row, t, k, t_ids_row), t_own[k])

            for i in range(-8, 0):
                if begins(i, -8) is not None:
                    adj_of(0, i, -8)
                if begins(i, -2) is not None and i + 2 >= 0:
                    own_of(0, i, -2)

            def steps(b, a, bG, i, known):
                if i == 0:
                    wait_alone(pool, g_listed, b + 1)
                if begins(i, -8) is not None and known(i, -8):
                    adj_of(b, i, -8)
                if begins(i, -2) is not None and known(i, -2):
                    own_of(b, i, -2)
                if known(i):
                    k, c = tile_of(i)
                    wait_alone(pool, t_idx, bG + i + 1)
                    if known(i, RING):
                        wait_alone(pool, t_pre, bG + i - RING + 1)
                    at = i % RING * SLOTS
                    def slot(j, done):
                        rows_of(msg_j, gathered[:, at + j, :], index[:, i, j:j + 1], done)
                    if (k, c) not in MAYBE:
                        for j in range(SLOTS):
                            slot(j, t_rows[i % RING])
                    else:
                        m = MAYBE.index((k, c))
                        longest = pool.value_load(longest_i[0:1, LONGEST, bass.ds(b, 1), k], min_val=0, max_val=N)
                        with pool.If(longest > c * SLOTS):
                            slot(0, t_maybe[m])
                            for j in range(1, SLOTS):
                                with pool.If(longest > c * SLOTS + j):
                                    slot(j, t_maybe[m])
                k = ends(i, 3)
                if k is not None and known(i, 3):
                    d = (i - 3) // G
                    over = pool.value_load(longest_i[0:1, OVER, bass.ds(b + d, 1), k], min_val=0, max_val=2 * N // SLOTS)
                    with pool.If(over > 0):
                        with pool.Fori(0, over):
                            n = pool.snap(seen)
                            wait_alone(pool, o_idx, n + 1)
                            for j in range(SLOTS):
                                rows_of(msg_j, o_pre[:, j, :], o_index[:, j:j + 1], o_dma)
                            wait_alone(pool, o_dma, (n + 1) * (16 * SLOTS))
                            pool.sem_inc(o_rows, 1)
                            pool.reg_add(seen, seen, 1)
                k = ends(i, 12)
                if k is not None and known(i, 12):
                    t = tiles_before(b, i, 12)
                    wait_alone(pool, e_out, t + 1)
                    pool.indirect_dma_start(out_flat, bass.IndirectOffsetOnAxis(ap=ids_row[:, k:k + 1], axis=0), out_sb[:, k % 2, :],
                                            None).then_inc(e_store[k % 2], 16)

            chunk_loop(pool, steps, G + 12)
            for q in range(2):
                pool.wait_ge(e_store[q], 16 * (TILES // 2))

        @block.scalar
        def _(act):
            def piece(a, i, alone):
                first = isinstance(a, int) and a == 0
                if i in (1, 2):
                    if i == 1:
                        act.wait_ge(g_load, (a + 1) * 32)
                        if not first:
                            act.wait_ge(g_nv, a * 2)
                    for it in (2 * i - 2, 2 * i - 1):
                        last = act.activation(junk_a[:, it, :], adj_g[:, it, :], ACT.Identity, accum_out=deg[:, it:it + 1])
                    if i == 2:
                        last.then_inc(g_deg, 1)
                if i == 1:
                    act.wait_ge(g_xT, a + 1)
                    if not first:
                        act.wait_ge(g_sup, a)
                    act.copy(xT[:, :], o_ps[:, 0, :]).then_inc(g_xTc, 1)
                if i in (2, 3, 4, 5):
                    act.wait_ge(g_adjT, a * 4 + (i - 1))
                    if i == 2 and not first:
                        act.wait_ge(g_prod, a)
                    act.copy(adjT[:, i - 2, :], o_ps[:, 0, :]).then_inc(g_adjTc, 1)
                if i == 16:
                    act.wait_ge(g_hT, a + 1)
                    if not first:
                        act.wait_ge(g_m, a * 2)
                    act.copy(hT[:, :], o_ps[:, 0, :]).then_inc(g_hTc, 1)
                if i == 17:
                    act.wait_ge(g_m, a * 2 + 1)
                    if not first:
                        act.wait_ge(g_store, a * 32)
                    act.copy(mj_g[:, :, :], o_ps[:, 0, :].rearrange("p (t o) -> p t o", t=TB)).then_inc(g_mj, 1)

            prepare_first(piece)
            act.wait_ge(s_zero, 3)

            seen = act.alloc_register("act_overflow_seen")
            act.reg_mov(seen, 0)

            def steps(b, a, bG, i, known):
                if i == 0:
                    act.wait_ge(g_listed, b + 1)
                if known(i):
                    act.wait_ge(t_pre, bG + i + 1)
                    if known(i, RG):
                        act.wait_ge(t_rs, (bG + i - RG + 1) * (STEPS + 1))
                        act.wait_ge(t_ssq, bG + i - RG + 1)
                    for j in range(SLOTS):
                        last = act.activation(squares[:, i % RG, j, :], pre[:, i % RG, j, :], ACT.Square,
                                              accum_out=ssq[:, i % RG, j:j + 1])
                    last.then_inc(t_ssq, 1)
                k = ends(i, 4)
                if k is not None and known(i, 4):
                    t = tiles_before(b, i, 4)
                    act.wait_ge(t_sum, t + 1)
                    if not (isinstance(t, int) and t == 0):
                        act.wait_ge(e_T, t)
                    act.copy(agg_sb[:, :, :], agg_ps[k % 2][:, 0, :].rearrange("p (k o) -> p k o", k=4)).then_inc(e_agg, 1)
                k = begins(i, -7)
                if k is not None and known(i, -7):
                    d = (i + 7) // G
                    t = tiles_before(b, i, -7)
                    act.wait_ge(t_adj[k], (b + d + 1) * 16)
                    if not (isinstance(t, int) and t < TB):
                        act.wait_ge(t_over, t - TB + 1)
                    act.activation(key[:, k, :], adj_t[:, k, :], ACT.Relu).then_inc(t_key, 1)
                if known(i, 2):
                    act.wait_ge(t_zt, bG + i - 1)
                    if known(i, 2 + RG):
                        act.wait_ge(t_zb, bG + i - 1 - RG)
                    act.activation(msgT[:, (i - 2) % RG, :, :], zt_ps[:, :, :].rearrange("p h (s n) -> p (h s) n", s=4),
                                   ACT.Gelu, bias=cols[:, 1:2], scale=cols[:, 0:1]).then_inc(t_gelu, 1)
                if known(i, 1):
                    act.wait_ge(t_rs, (bG + i) * (STEPS + 1))
                    for j in range(SLOTS):
                        r = (i - 1) % RG
                        last = act.activation(pre[:, r, j, :], pre[:, r, j, :], ACT.Identity, scale=rstd[:, r, j:j + 1])
                    last.then_inc(t_scaled, 1)
                if a is not None:
                    piece(a, i, False)
                k = ends(i, 5)
                if k is not None and known(i, 5):
                    act.wait_ge(e_T, tiles_before(b, i, 5) + 1)
                    act.copy(endT[:, :, :], end_ps[:, 0, 0:2 * P].rearrange("p (a n) -> p a n", a=2)).then_inc(e_Tc, 1)
                k = ends(i, 3)
                if k is not None and known(i, 3):
                    d = (i - 3) // G
                    over = act.value_load(longest_i[0:1, OVER, bass.ds(b + d, 1), k], min_val=0, max_val=2 * N // SLOTS)
                    with act.If(over > 0):
                        with act.Fori(0, over):
                            n = act.snap(seen)
                            act.wait_ge(o_prep, n + 1)
                            for j in range(SLOTS):
                                last = act.activation(o_squares[:, j, :], o_pre[:, j, :], ACT.Square, accum_out=o_ssq[:, j:j + 1])
                            last.then_inc(o_sums, 1)
                            act.wait_ge(o_root, n + 1)
                            for j in range(SLOTS):
                                last = act.activation(o_pre[:, j, :], o_pre[:, j, :], ACT.Identity, scale=o_rstd[:, j:j + 1])
                            last.then_inc(o_scaled, 1)
                            for half in range(2):
                                act.wait_ge(o_zt, 2 * n + half + 1)
                                act.activation(o_msgT[:, 4 * half:4 * half + 4, :], o_ps[:, 0, :].rearrange("p (s n) -> p s n", s=4),
                                               ACT.Gelu, bias=cols[:, 1:2], scale=cols[:, 0:1]).then_inc(o_gelu, 1)
                            act.reg_add(seen, seen, 1)

            chunk_loop(act, steps, G + 6, lead=7)

        @block.vector
        def _(dve):
            done = [0]

            def step(ins):
                done[0] += 1
                ins.then_inc(s_seq, 1)
                dve.wait_ge(s_seq, done[0])

            def rsqrt_step(j, v, ii, uu, y):
                if j == 0:
                    return dve.tensor_scalar(ii, v.bitcast(U32), 1, None, ALU.logical_shift_right)
                if j == 1:
                    return dve.tensor_scalar(y.bitcast(U32), ii, -1.0, MAGIC, ALU.mult, ALU.add)
                if j % 3 == 2:
                    return dve.scalar_tensor_tensor(uu, y, -0.5, y, ALU.mult, ALU.mult)
                if j % 3 == 0:
                    return dve.tensor_tensor(uu, uu, v, ALU.mult)
                return dve.scalar_tensor_tensor(y, uu, 1.5, y, ALU.add, ALU.mult)

            dve.wait_ge(s_const, 16 * N_CONST)
            dve.wait_ge(s_ident, 2)
            dve.wait_ge(s_iota, 4)
            for k in range(2):
                step(dve.reduce_sum(mean1[:, k:k + 1], w1_sb[:, k, :], AX.X))
            step(dve.reduce_sum(mean1[:, 2:3], b1_all, AX.X))
            step(dve.tensor_scalar(mean1[:, :], mean1[:, :], -1.0 / D, None, ALU.mult))
            for k in range(2):
                step(dve.tensor_scalar(w1_sb[:, k, :], w1_sb[:, k, :], mean1[:, k:k + 1], None, ALU.add))
            step(dve.tensor_scalar(b1_all, b1_all, mean1[:, 2:3], None, ALU.add))
            step(dve.tensor_scalar(cols[:, 0:1], cols[:, 0:1], ROOT_D, None, ALU.mult))
            step(dve.tensor_scalar(g2_all, g2_all, ROOT_D, None, ALU.mult))
            step(dve.tensor_copy(rest[:, :], b2_all))
            for k in range(3):
                step(dve.tensor_copy(parts[:, k, :], rest[:, :]))
                step(dve.tensor_tensor(rest[:, :], rest[:, :], parts[:, k, :], ALU.subtract))
            step(dve.tensor_scalar(b2_split[:, :], parts[0:3, 0, :], ident[0:3, 0:1], None, ALU.mult))
            for k in (1, 2):
                step(dve.scalar_tensor_tensor(b2_split[:, :], parts[0:3, k, :], ident[0:3, k:k + 1], b2_split[:, :], ALU.mult, ALU.add))
            step(dve.memset(ones3[:, :], 1.0))
            step(dve.memset(ones[:, :], 1.0))
            step(dve.memset(summed[:, :], 0.0))
            step(dve.memset(rs_v[:, :], 1.0))
            step(dve.tensor_copy(facts[:, :, 0], number[:, :]))
            for k in range(TB):
                step(dve.memset(whole[:, 0, k:k + 1], float(CHUNKS[k] * SLOTS)))
                step(dve.memset(whole[:, 1, k:k + 1], float(SLOTS - 1 - CHUNKS[k] * SLOTS)))
            dve.sem_inc(s_setup, 1)

            TABLE_STEPS = 11

            def piece(a, i, alone):
                first = isinstance(a, int) and a == 0
                r = 0 if alone else (i - 1) % RG

                def root(lo, hi, n):
                    dve.wait_ge(g_nv, 2 * a + n + 1)
                    for j in range(STEPS):
                        if j:
                            dve.wait_ge(g_rs, (2 * a + n) * STEPS + j)
                        rsqrt_step(j, rs_v[:, lo:hi], rs_i[:, lo:hi], rs_u[:, lo:hi], rstd[:, 0, lo:hi]).then_inc(g_rs, 1)
                    dve.wait_ge(g_rs, (2 * a + n + 1) * STEPS)

                if i == 0:
                    dve.wait_ge(g_load, (a + 1) * 32)
                    if not first:
                        dve.wait_ge(g_pre, a)
                    dve.tensor_tensor(xb_g[:, :, :], x_g[:, :, :], b0_all.unsqueeze(1).to_broadcast([P, TB, D]), ALU.add).then_inc(g_xb, 1)
                if i in (1, 2, 3, 4):
                    if i == 1 and not first:
                        dve.wait_ge(g_order, a)
                        dve.wait_ge(g_key, a)
                    for it in range(TB)[2 * ((i - 1) % 2):][:2]:
                        if i < 3:
                            last = dve.tensor_scalar(junk_v[:, 0, it, :], adj_g[:, it, :], 0.0, 0.0, ALU.is_gt, ALU.add,
                                                     accum_out=facts[:, it, 1:2])
                        else:
                            last = dve.tensor_scalar(junk_v[:, 1, it, :], adj_g[:, it, :], 0.0, 0.0, ALU.is_lt, ALU.add,
                                                     accum_out=negative[:, it:it + 1])
                    if i in (2, 4):
                        last.then_inc(g_count, 1)
                if i == 4:
                    dve.wait_ge(g_count, a * 2 + 2)
                    if not first:
                        dve.wait_ge(g_rank, a)
                    dve.scalar_tensor_tensor(sort_key[:, :], facts[:, :, 1], float(N), backward[:, :], ALU.mult, ALU.add).then_inc(g_key, 1)
                    dve.wait_ge(g_deg, a + 1)
                    dve.tensor_scalar(rs_v[:, DEG:VAR], deg[:, :], 1.0, None, ALU.add).then_inc(g_nv, 1)
                    if alone:
                        root(DEG, VAR, 0)
                if i == 5:
                    dve.wait_ge(g_nv, a * 2 + 1)
                    if not first:
                        dve.wait_ge(g_dis, a)
                        dve.wait_ge(g_pre, a)
                    dve.tensor_scalar(nonzero[:, :], rs_v[:, DEG:VAR], 0.0, None, ALU.not_equal).then_inc(g_mask, 1)
                    dve.wait_ge(g_mask, a + 1)
                    dve.tensor_tensor(dis[:, :], rstd[:, r, DEG:VAR], nonzero[:, :], ALU.mult).then_inc(g_dis, 1)
                if i == 6:
                    dve.wait_ge(g_dis, a + 1)
                    if not first:
                        dve.wait_ge(g_prod, a)
                    dve.wait_ge(g_sup, a + 1)
                    dve.tensor_tensor(sup[:, :, :], o_ps[:, 0, :].rearrange("p (t d) -> p t d", t=TB),
                                      dis[:, :].unsqueeze(2).to_broadcast([P, TB, D]), ALU.mult).then_inc(g_supc, 1)
                if i == 7:
                    dve.wait_ge(g_keys, a + 1)
                    if not first:
                        dve.wait_ge(g_chosen, a)
                    for it in range(TB):
                        last = dve.tensor_scalar(junk_v[:, 2, it, :], o_ps[:, 0, :], sort_key[:, it:it + 1], 0.0, ALU.is_gt, ALU.add,
                                                 accum_out=rank[:, it:it + 1])
                    last.then_inc(g_rank, 1)
                if i == 8:
                    dve.wait_ge(g_rank, a + 1)
                    if not first:
                        dve.wait_ge(g_order, a)
                    for it in range(TB):
                        last = dve.tensor_scalar(chosen[:, it, :], places[:, :], rank[:, it:it + 1], None, ALU.is_equal)
                    last.then_inc(g_chosen, 1)
                if i == 9:
                    dve.wait_ge(g_order, a + 1)
                    if not first:
                        dve.wait_ge(g_table, a * TABLE_STEPS)
                    dve.tensor_scalar(row_id[:, bass.ds(a * TB, TB)], o_ps[:, 0, 0:2 * TB].rearrange("p (k f) -> p k f", f=2)[:, :, 0],
                                      base[:, bass.ds(a * TB, 1)], None, ALU.add)
                    dve.tensor_copy(longest_f[:, :], o_ps[0:1, 0, 0:2 * TB].rearrange("p (k f) -> p k f", f=2)[:, :, 1])
                    dve.reduce_sum(neg_f[:, :], o_ps[0:1, 0, 2 * TB:3 * TB], AX.X).then_inc(g_ids, 1)
                if i == 10:
                    dve.wait_ge(g_ids, a + 1)
                    made = [0]
                    def link(ins):
                        made[0] += 1
                        ins.then_inc(g_table, 1)
                        dve.wait_ge(g_table, a * TABLE_STEPS + made[0])
                    def entry(k):
                        return longest_i[:, k, bass.ds(a, 1), :].rearrange("p b k -> p (b k)")
                    dve.tensor_copy(entry(LONGEST), longest_f[:, :])
                    for m, (k, c) in enumerate(MAYBE):
                        dve.tensor_scalar(sized[:, m:m + 1], longest_f[:, k:k + 1], float(-c * SLOTS), 0.0, ALU.add, ALU.max)
                    link(dve.tensor_tensor(pos_f[:, :], longest_f[:, :], whole[:, 0, :], ALU.max))
                    link(dve.tensor_scalar(sized[:, :], sized[:, :], float(SLOTS), 16.0, ALU.min, ALU.mult))
                    link(dve.tensor_tensor(summed[:, :], summed[:, :], sized[:, :], ALU.add))
                    dve.tensor_copy(arrivals[:, :, bass.ds(a, 1)].rearrange("p m b -> p (m b)"), summed[:, :])
                    link(dve.tensor_tensor(over_i[:, 0, :], pos_f[:, :], whole[:, 1, :], ALU.add))
                    link(dve.tensor_scalar(neg_f[:, :], neg_f[:, :], float(N), float(SLOTS - 1), ALU.min, ALU.add))
                    link(dve.tensor_copy(over_i[:, 1, :], neg_f[:, :].to_broadcast([1, TB])))
                    link(dve.tensor_scalar(over_i[:, 0:2, :], over_i[:, 0:2, :], 3, None, ALU.logical_shift_right))
                    dve.sem_inc(s_carrier[dve.engine], 1)
                    link(dve.tensor_tensor(over_i[:, 2, :], over_i[:, 0, :], over_i[:, 1, :], ALU.add))
                    for n, k in enumerate((OVER_POS, OVER_NEG, OVER)):
                        link(dve.tensor_copy(entry(k), over_i[:, n, :]))
                    assert made[0] == TABLE_STEPS
                    dve.sem_inc(g_listed, 1)
                if i == 13:
                    dve.wait_ge(g_prod, a + 1)
                    dve.wait_ge(g_xb, a + 1)
                    if not first:
                        dve.wait_ge(g_h, a)
                    for it in range(TB):
                        last = dve.scalar_tensor_tensor(pre_g[:, it, :], o_ps[:, 0, it * D:(it + 1) * D], dis[:, it:it + 1],
                                                        xb_g[:, it, :], ALU.mult, ALU.add)
                    last.then_inc(g_pre, 1)
                    dve.wait_ge(g_pre, a + 1)
                    for it in range(TB):
                        last = dve.bn_stats(stats_g[:, it, :], pre_g[:, it, :])
                    last.then_inc(g_stats, 1)
                    wait_alone(dve, g_stats, a * 2 + 1)
                    for it in range(TB):
                        last = dve.bn_aggr(mv_g[:, it, :], stats_g[:, it, :])
                    last.then_inc(g_stats, 1)
                    dve.wait_ge(g_stats, a * 2 + 2)
                    dve.tensor_scalar(rs_v[:, VAR:ROOTS], mv_g[:, :, 1], EPS, None, ALU.add).then_inc(g_nv, 1)
                    if alone:
                        root(VAR, ROOTS, 1)
                if i == 14:
                    if not first:
                        dve.wait_ge(g_store, a * 32)
                    for it in range(TB):
                        last = dve.tensor_scalar(own_g[:, it, 0:D], pre_g[:, it, :], mv_g[:, it, 0:1],
                                                 rstd[:, r, VAR + it:VAR + it + 1], ALU.subtract, ALU.mult)
                    last.then_inc(g_h, 1)
                if i == 18:
                    dve.wait_ge(g_m, a * 2 + 2)
                    dve.tensor_tensor(own_g[:, :, D:2 * D], o_ps[:, 0, :].rearrange("p (t o) -> p t o", t=TB),
                                      b1_all.unsqueeze(1).to_broadcast([P, TB, D]), ALU.add).then_inc(g_mi, 1)

            prepare_first(piece)
            dve.wait_ge(s_zero, 3)

            seen = dve.alloc_register("dve_overflow_seen")
            dve.reg_mov(seen, 0)

            def steps(b, a, bG, i, known):
                if i == 0:
                    dve.wait_ge(g_table, (b + 1) * TABLE_STEPS)
                if known(i):
                    k, c = tile_of(i)
                    if c == 0:
                        dve.wait_ge(t_own[k], 16 * (b + 1))
                    if (k, c) not in MAYBE:
                        r = i % RING
                        others = [j for j in range(G) if j % RING == r and tile_of(j) not in MAYBE]
                        dve.wait_ge(t_rows[r], (b * len(others) + others.index(i) + 1) * (16 * SLOTS))
                    else:
                        longest = dve.value_load(longest_i[0:1, LONGEST, bass.ds(b, 1), k], min_val=0, max_val=N)
                        with dve.If(longest > c * SLOTS):
                            m = MAYBE.index((k, c))
                            value = dve.value_load(arrivals[0:1, m, bass.ds(b, 1)], min_val=16, max_val=16 * SLOTS * B)
                            wait_alone(dve, t_maybe[m], value)
                    if known(i, RG):
                        dve.wait_ge(t_zt, bG + i - RG + 1)
                    dve.tensor_tensor(pre[:, i % RG, :, :], gathered[:, i % RING * SLOTS:(i % RING + 1) * SLOTS, :],
                                      own_t[:, k, D:2 * D].unsqueeze(1).to_broadcast([P, SLOTS, D]), ALU.add).then_inc(t_pre, 1)
                k1 = ends(i, 7) if known(i, 7) else None
                k2 = ends(i, 8) if known(i, 8) else None
                def link(e, ins, n):
                    ins.then_inc(e_seq, 1)
                    dve.wait_ge(e_seq, e * E_STEPS + n)
                if k1 is not None:
                    e = tiles_before(b, i, 7)
                    dve.wait_ge(e_upd, e + 1)
                    link(e, dve.bn_stats(stats[:, :], end_ps[:, 0, 2 * P:3 * P]), 1)
                    dve.sem_inc(s_carrier[dve.engine], 1)
                    link(e, dve.bn_aggr(mv[:, :], stats[:, :]), 2)
                    link(e, dve.tensor_scalar(ssq[:, (i - 1) % RG, SLOTS:], mv[:, 1:2], float(D), None, ALU.mult), 3)
                if known(i, -AHEAD):
                    s, sk = bG + i + AHEAD, tile_of(i + AHEAD)[0]
                    si = (i + AHEAD) % G
                    if begins(i, -AHEAD) is not None:
                        wait_alone(dve, t_key, tiles_before(b, i, -AHEAD) + 1)
                    else:
                        wait_alone(dve, t_zap, s)
                    dve.max(weight[:, si, :], key[:, sk, :]).then_inc(t_max, 1)
                if known(i, 1) or i > G:
                    r = (i - 1) % RG
                    if known(i, 1):
                        dve.wait_ge(t_ssq, bG + i)
                    if k1 is not None:
                        dve.wait_ge(e_seq, e * E_STEPS + 3)
                    if k2 is not None:
                        dve.wait_ge(e_var, tiles_before(b, i, 8) + 1)
                    if a is not None and i in (5, 14):
                        dve.wait_ge(g_nv, a * 2 + (1 if i == 5 else 2))
                    dve.tensor_scalar(rs_v[:, 0:DEG], ssq[:, r, :], D * EPS, None, ALU.add).then_inc(t_rs, 1)
                    for j in range(STEPS):
                        dve.wait_ge(t_rs, (bG + i - 1) * (STEPS + 1) + j + 1)
                        rsqrt_step(j, rs_v[:, :], rs_i[:, :], rs_u[:, :], rstd[:, r, :]).then_inc(t_rs, 1)
                if known(i, -AHEAD):
                    wait_alone(dve, t_max, s + 1)
                    dve.max_index(found[:, si, :], weight[:, si, :], key[:, sk, :]).then_inc(t_find, 1)
                    dve.match_replace(out=key[:, sk, :], in_to_replace=weight[:, si, :], in_values=key[:, sk, :],
                                      imm_value=0.0).then_inc(t_zap, 1)
                    dve.wait_ge(t_find, s + 1)
                    first_row = base[:, bass.ds(tiles_before(b, i, -AHEAD), 1)]
                    dve.tensor_scalar(index[:, si, :], found[:, si, :], first_row, None, ALU.add).then_inc(t_idx, 1)
                if k1 is not None:
                    dve.wait_ge(t_rs, (bG + i) * (STEPS + 1))
                    link(e, dve.tensor_scalar(upd[:, :], end_ps[:, 0, 2 * P:3 * P], mv[:, 0:1], rstd[:, (i - 1) % RG, SLOTS:DEG],
                                              ALU.subtract, ALU.mult), 4)
                    link(e, dve.tensor_tensor(upd[:, :], upd[:, :], g2_all, ALU.mult), 5)
                    link(e, dve.tensor_tensor(res[:, :], own_t[:, k1, 0:D], be2_all, ALU.add), 6)
                    link(e, dve.tensor_tensor(res[:, :], res[:, :], upd[:, :], ALU.add), 7)
                    link(e, dve.bn_stats(stats[:, :], res[:, :]), 8)
                    dve.sem_inc(s_carrier[dve.engine], 1)
                    link(e, dve.bn_aggr(mv[:, :], stats[:, :]), 9)
                    dve.tensor_scalar(ssq[:, i % RG, SLOTS:], mv[:, 1:2], float(D), None, ALU.mult).then_inc(e_var, 1)
                if k2 is not None:
                    e = tiles_before(b, i, 8)
                    dve.wait_ge(t_rs, (bG + i) * (STEPS + 1))
                    dve.tensor_scalar(r_end[:, :], rstd[:, (i - 1) % RG, SLOTS:DEG], ROOT_D, None, ALU.mult).then_inc(e_root, 1)
                    dve.wait_ge(e_root, e + 1)
                    if not (isinstance(e, int) and e < 2):
                        dve.wait_ge(e_store[k2 % 2], 8 * (e - k2 % 2))
                    dve.tensor_scalar(out_sb[:, k2 % 2, :], res[:, :], mv[:, 0:1], r_end[:, :], ALU.subtract, ALU.mult).then_inc(e_out, 1)
                if a is not None:
                    if i in (5, 14):
                        dve.wait_ge(t_rs, (bG + i) * (STEPS + 1))
                    piece(a, i, False)
                if known(i, 3):
                    dve.wait_ge(t_zb, bG + i - 2)
                    if known(i, 3 + RG):
                        dve.wait_ge(t_agg, bG + i - 2 - RG)
                    dve.tensor_tensor(msg[:, i % RG, :, :], zb_ps[:, :, :].rearrange("p h (s o) -> p (h s) o", s=4),
                                      weight[:, (i - 3) % G, :].unsqueeze(2).to_broadcast([P, SLOTS, D]), ALU.mult).then_inc(t_wmsg, 1)
                k = ends(i, 3)
                if k is not None and known(i, 3):
                    g = b + (i - 3) // G
                    wait_alone(dve, t_wmsg, bG + i - 2)
                    over = dve.value_load(longest_i[0:1, OVER_POS, bass.ds(g, 1), k], min_val=0, max_val=N // SLOTS)
                    with dve.If(over > 0):
                        with dve.Fori(0, over):
                            overflow_chunk(g, k, 1.0)
                    over = dve.value_load(longest_i[0:1, OVER_NEG, bass.ds(g, 1), k], min_val=0, max_val=N // SLOTS)
                    with dve.If(over > 0):
                        dve.tensor_scalar(key[:, k, :], adj_t[:, k, :], -1.0, 0.0, ALU.mult, ALU.max).then_inc(o_key, 1)
                        dve.wait_ge(o_key, 1)
                        dve.sem_clear(o_key)
                        with dve.Fori(0, over):
                            overflow_chunk(g, k, -1.0)
                    dve.sem_inc(t_over, 1)

            O_STEPS = 6 + STEPS

            def overflow_chunk(g, k, sign):
                n = dve.snap(seen)
                count = [0]
                def link(ins):
                    count[0] += 1
                    ins.then_inc(o_seq, 1)
                    wait_alone(dve, o_seq, n * O_STEPS + count[0])
                link(dve.max(o_weight[:, :], key[:, k, :]))
                link(dve.max_index(o_found[:, :], o_weight[:, :], key[:, k, :]))
                link(dve.match_replace(out=key[:, k, :], in_to_replace=o_weight[:, :], in_values=key[:, k, :], imm_value=0.0))
                link(dve.tensor_scalar(o_weight[:, :], o_weight[:, :], sign, None, ALU.mult))
                dve.tensor_scalar(o_index[:, :], o_found[:, :], base[:, bass.ds(g * TB, 1)], None, ALU.add).then_inc(o_idx, 1)
                dve.wait_ge(o_rows, n + 1)
                link(dve.tensor_tensor(o_pre[:, :, :], o_pre[:, :, :], own_t[:, k, D:2 * D].unsqueeze(1).to_broadcast([P, SLOTS, D]), ALU.add))
                dve.sem_inc(o_prep, 1)
                dve.wait_ge(o_sums, n + 1)
                link(dve.tensor_scalar(o_ssq[:, :], o_ssq[:, :], D * EPS, None, ALU.add))
                for j in range(STEPS):
                    link(rsqrt_step(j, o_ssq[:, :], rs_i[:, 0:SLOTS], rs_u[:, 0:SLOTS], o_rstd[:, :]))
                dve.sem_inc(o_root, 1)
                for half in range(2):
                    dve.wait_ge(o_zb, 2 * n + half + 1)
                    at = slice(4 * half, 4 * half + 4)
                    dve.tensor_tensor(o_msg[:, at, :], o_ps[:, 0, :].rearrange("p (s o) -> p s o", s=4),
                                      o_weight[:, at].unsqueeze(2).to_broadcast([P, 4, D]), ALU.mult).then_inc(o_wmsg, 1)
                dve.wait_ge(o_agg, n + 1)
                dve.reg_add(seen, seen, 1)

            chunk_loop(dve, steps, G + 8, lead=AHEAD)

        @block.tensor
        def _(pe):
            pe.wait_ge(s_ident, 2)
            pe.wait_ge(s_setup, 1)
            mm, transpose = nc.tensor.matmul, nc.tensor.transpose

            def piece(a, i, alone):
                first = isinstance(a, int) and a == 0
                o = o_ps[:, 0, :]
                if i == 0:
                    pe.wait_ge(g_load, (a + 1) * 32)
                    if not first:
                        pe.wait_ge(g_mi, a)
                    for it in range(TB):
                        last = transpose(o[:, it * P:(it + 1) * P], x_g[:, it, :], ident[:, :])
                    last.then_inc(g_xT, 1)
                if i in (1, 2, 3, 4):
                    if i == 1:
                        pe.wait_ge(g_xTc, a + 1)
                    else:
                        pe.wait_ge(g_adjTc, a * 4 + (i - 1))
                    mt = i - 1
                    for it in range(TB):
                        last = transpose(o[:, it * P:(it + 1) * P], adj_g[:, it, mt * P:(mt + 1) * P], ident[:, :])
                    last.then_inc(g_adjT, 1)
                if i == 5:
                    pe.wait_ge(g_adjTc, a * 4 + 4)
                    for it in range(TB):
                        last = mm(o[:, it * D:(it + 1) * D], xT[:, it * P:(it + 1) * P], w0_sb[:, :], start=True, stop=True)
                    last.then_inc(g_sup, 1)
                if i == 6:
                    pe.wait_ge(g_key, a + 1)
                    pe.wait_ge(g_supc, a + 1)
                    for it in range(TB):
                        last = mm(o[:, it * P:(it + 1) * P], sort_key[:, it:it + 1].to_broadcast([P, P]), ident[:, :],
                                  start=True, stop=True)
                    last.then_inc(g_keys, 1)
                if i == 8:
                    pe.wait_ge(g_chosen, a + 1)
                    for k in range(TB):
                        for it in range(TB):
                            mm(o[:, 2 * k:2 * k + 2], chosen[:, it, k * P:(k + 1) * P], facts[:, it, :],
                               start=(it == 0), stop=(it == TB - 1))
                    mm(o[:, 2 * TB:3 * TB], ones[:, :], negative[:, :], start=True, stop=True).then_inc(g_order, 1)
                if i in (9, 10, 11, 12):
                    if i == 9:
                        pe.wait_ge(g_ids, a + 1)
                    it = i - 9
                    dst = o[:, it * D:(it + 1) * D]
                    for mt in range(TB):
                        mm(dst, adjT[:, mt, it * P:(it + 1) * P], sup[:, mt, :], start=(mt == 0), stop=False)
                    last = mm(dst, ident[:, :], sup[:, it, :], start=False, stop=True)
                    if i == 12:
                        last.then_inc(g_prod, 1)
                if i == 15:
                    pe.wait_ge(g_h, a + 1)
                    for it in range(TB):
                        last = transpose(o[:, it * P:(it + 1) * P], own_g[:, it, 0:D], ident[:, :])
                    last.then_inc(g_hT, 1)
                if i in (16, 17):
                    if i == 16:
                        pe.wait_ge(g_hTc, a + 1)
                    else:
                        pe.wait_ge(g_mj, a + 1)
                    for it in range(TB):
                        last = mm(o[:, it * D:(it + 1) * D], hT[:, it * P:(it + 1) * P], w1_sb[:, i - 16, :], start=True, stop=True)
                    last.then_inc(g_m, 1)

            prepare_first(piece)

            seen = pe.alloc_register("pe_overflow_seen")
            pe.reg_mov(seen, 0)

            def steps(b, a, bG, i, known):
                if i == 0:
                    pe.wait_ge(g_listed, b + 1)
                k = ends(i, 6)
                if k is not None and known(i, 6):
                    pe.wait_ge(e_Tc, tiles_before(b, i, 6) + 1)
                    u = end_ps[:, 0, 2 * P:3 * P]
                    mm(u, endT[:, 1, :], w2_sb[:, 0, :], start=True, stop=False)
                    mm(u, endT[:, 0, :], w2_sb[:, 1, :], start=False, stop=False)
                    mm(u, ones3[:, :], b2_split[:, :], start=False, stop=True).then_inc(e_upd, 1)
                if known(i, 1):
                    pe.wait_ge(t_scaled, bG + i)
                    if known(i, 2):
                        pe.wait_ge(t_gelu, bG + i - 1)
                    for j in range(SLOTS):
                        last = transpose(zt_ps[:, j // 4, j % 4 * P:(j % 4 + 1) * P], pre[:, (i - 1) % RG, j, :], ident[:, :])
                    last.then_inc(t_zt, 1)
                if known(i, 2):
                    pe.wait_ge(t_gelu, bG + i - 1)
                    if known(i, 3):
                        pe.wait_ge(t_wmsg, bG + i - 2)
                    for j in range(SLOTS):
                        last = transpose(zb_ps[:, j // 4, j % 4 * D:(j % 4 + 1) * D], msgT[:, (i - 2) % RG, j, :], ident[:, :])
                    last.then_inc(t_zb, 1)
                if known(i, 3):
                    k, c = tile_of(i - 3)
                    t = tiles_before(b, i, 3)
                    pe.wait_ge(t_wmsg, bG + i - 2)
                    if c == 0 and not (isinstance(t, int) and t < 2):
                        pe.wait_ge(e_agg, t - 1)
                    for half in range(2):
                        last = mm(agg_ps[k % 2][:, 0, :], ident[:, :], msg[:, i % RG, 4 * half:4 * half + 4, :].rearrange("p s o -> p (s o)"),
                                  start=(c == 0 and half == 0), stop=True, skip_group_check=True)
                    last.then_inc(t_agg, 1)
                k = ends(i, 4)
                if k is not None and known(i, 4):
                    t = tiles_before(b, i, 4)
                    pe.wait_ge(e_agg, t + 1)
                    if not (isinstance(t, int) and t == 0):
                        pe.wait_ge(e_seq, (t - 1) * E_STEPS + 4)
                    for s4 in range(4):
                        mm(end_ps[:, 0, 0:P], agg_sb[:, s4, :], ident[:, :], start=(s4 == 0), stop=(s4 == 3))
                    transpose(end_ps[:, 0, P:2 * P], own_t[:, k, 0:D], ident[:, :]).then_inc(e_T, 1)
                k = ends(i, 3)
                if k is not None and known(i, 3):
                    d = (i - 3) // G
                    over = pe.value_load(longest_i[0:1, OVER, bass.ds(b + d, 1), k], min_val=0, max_val=2 * N // SLOTS)
                    with pe.If(over > 0):
                        if a is None:
                            wait_alone(pe, g_mi, B)
                        elif i == 2:
                            wait_alone(pe, g_adjTc, a * 4 + 1)
                        elif i == 9:
                            wait_alone(pe, g_ids, a + 1)
                        elif i == 14:
                            wait_alone(pe, g_pre, a + 1)
                        else:
                            assert i == 19
                            wait_alone(pe, g_mi, a + 1)
                        with pe.Fori(0, over):
                            n = pe.snap(seen)
                            pe.wait_ge(o_scaled, n + 1)
                            for half in range(2):
                                if half:
                                    pe.wait_ge(o_wmsg, 2 * n + 1)
                                for j in range(4):
                                    last = transpose(o_ps[:, 0, j * P:(j + 1) * P], o_pre[:, 4 * half + j, :], ident[:, :])
                                last.then_inc(o_zt, 1)
                                pe.wait_ge(o_gelu, 2 * n + half + 1)
                                for j in range(4):
                                    last = transpose(o_ps[:, 0, j * D:(j + 1) * D], o_msgT[:, 4 * half + j, :], ident[:, :])
                                last.then_inc(o_zb, 1)
                            pe.wait_ge(o_wmsg, 2 * n + 2)
                            for half in range(2):
                                last = mm(agg_ps[k % 2][:, 0, :], ident[:, :], o_msg[:, 4 * half:4 * half + 4, :].rearrange("p s o -> p (s o)"),
                                          start=False, stop=True, skip_group_check=True)
                            last.then_inc(o_agg, 1)
                            pe.wait_ge(o_agg, n + 1)
                            pe.reg_add(seen, seen, 1)
                    pe.wait_ge(t_agg, bG + i - 2)
                    pe.sem_inc(t_sum, 1)
                if a is not None:
                    piece(a, i, False)

            chunk_loop(pe, steps, G + 6)


INS = ["x", "adj", "L0_gnn_weight", "L0_gnn_bias", "L1_gnn_W1", "L1_gnn_b1", "L1_gnn_g1", "L1_gnn_be1",
       "L1_gnn_W2", "L1_gnn_b2", "L1_gnn_g2", "L1_gnn_be2"]


def kernel(**inputs):
    import concourse.bacc as bacc
    from concourse.bass_utils import run_bass_kernel_spmd

    nc = bacc.Bacc("TRN2", target_bir_lowering=False, num_devices=1)
    arrays = {f"in_{n}": np.ascontiguousarray(inputs[n]) for n in INS}
    args = [nc.dram_tensor(n, a.shape, mybir.dt.from_np(a.dtype), kind="ExternalInput").ap() for n, a in arrays.items()]
    out = nc.dram_tensor("out_0", (B, N, D), FP32, kind="ExternalOutput").ap()
    adj_resnorm_kernel(nc, *args, out)
    r = run_bass_kernel_spmd(nc, [arrays], core_ids=[0])
    return r.results[0]["out_0"]
```
